# Optimizing a Trainium2 kernel written in Bass

```python
import numpy as np
import jax
import jax.numpy as jnp

def _softmax(x, axis=-1):
    return jax.nn.softmax(x, axis=axis)

def _gelu(x):
    return jax.nn.gelu(x, approximate=True)

def _silu(x):
    return jax.nn.silu(x)

def _sigmoid(x):
    return jax.nn.sigmoid(x)

def _layernorm(x, axis=-1, eps=1e-05):
    m = jnp.mean(x, axis=axis, keepdims=True)
    v = jnp.var(x, axis=axis, keepdims=True)
    return (x - m) / jnp.sqrt(v + eps)

def _scatter_add(tgt, idx, src, axis=0):
    return tgt.at[idx].add(src)

def _segment_sum(src, seg, n):
    return jax.ops.segment_sum(src, seg, n)
kernel_name = 'mk_macaron_d1_jaxref_r8_92c561'

def setup_inputs(seed: int=0):
    np.random.seed(seed)
    _w = jnp.asarray

    def _L0_attn_setup():
        import jax, jax.numpy as jnp
        import numpy as np
        B, L, D_INNER, N_STATE, DT_RANK = (2, 128, 256, 16, 64)
        key = jax.random.key(seed)
        k0, k1, k2, k3 = jax.random.split(key, 4)
        x = jax.random.normal(k0, (B, L, D_INNER), dtype=jnp.float32)
        W_x = jax.random.normal(k1, (DT_RANK + 2 * N_STATE, D_INNER), dtype=jnp.float32) * 0.02
        W_dt = jax.random.uniform(k2, (D_INNER, DT_RANK), minval=-0.1, maxval=0.1, dtype=jnp.float32)
        inv_dt_min = float(np.log(np.expm1(0.001)))
        inv_dt_max = float(np.log(np.expm1(0.1)))
        b_dt = jax.random.uniform(k3, (D_INNER,), minval=inv_dt_min, maxval=inv_dt_max, dtype=jnp.float32)
        A_log = jnp.log(jnp.broadcast_to(jnp.arange(1, N_STATE + 1, dtype=jnp.float32), (D_INNER, N_STATE)))
        D = jnp.ones((D_INNER,), dtype=jnp.float32)
        return {'x': x, 'W_x': W_x, 'W_dt': W_dt, 'b_dt': b_dt, 'A_log': A_log, 'D': D}
    _L0_attn_in = _L0_attn_setup()

    def _L0_ffn_setup():
        import jax, jax.numpy as jnp
        import numpy as np
        SEQ, BS, D, F, E = (128, 2, 256, 256, 8)
        key = jax.random.key(seed)
        ks = jax.random.split(key, 8)
        s = 0.02
        return {'hidden_states': jax.random.normal(ks[0], (SEQ, BS, D), jnp.float32), 'router_w': jax.random.normal(ks[1], (D, E), jnp.float32) * s, 'gate_w': jax.random.normal(ks[2], (E, D, F), jnp.float32) * s, 'up_w': jax.random.normal(ks[3], (E, D, F), jnp.float32) * s, 'down_w': jax.random.normal(ks[4], (E, F, D), jnp.float32) * s, 'shared_gate_w': jax.random.normal(ks[5], (D, F), jnp.float32) * s, 'shared_up_w': jax.random.normal(ks[6], (D, F), jnp.float32) * s, 'shared_down_w': jax.random.normal(ks[7], (F, D), jnp.float32) * s}
    _L0_ffn_in = _L0_ffn_setup()
    _d = {'L0_attn_x': _L0_attn_in['x'], 'L0_attn_W_x': _L0_attn_in['W_x'], 'L0_attn_W_dt': _L0_attn_in['W_dt'], 'L0_attn_b_dt': _L0_attn_in['b_dt'], 'L0_attn_A_log': _L0_attn_in['A_log'], 'L0_attn_D': _L0_attn_in['D'], 'L0_ffn_router_w': _L0_ffn_in['router_w'], 'L0_ffn_gate_w': _L0_ffn_in['gate_w'], 'L0_ffn_up_w': _L0_ffn_in['up_w'], 'L0_ffn_down_w': _L0_ffn_in['down_w'], 'L0_ffn_shared_gate_w': _L0_ffn_in['shared_gate_w'], 'L0_ffn_shared_up_w': _L0_ffn_in['shared_up_w'], 'L0_ffn_shared_down_w': _L0_ffn_in['shared_down_w']}
    _x0 = _d['L0_attn_x']
    _d['L0_attn_x'] = jax.random.normal(jax.random.fold_in(jax.random.key(seed), 1), (4, 512, 256), dtype=_x0.dtype)
    del _x0
    return _d

def reference(L0_attn_x, L0_attn_W_x, L0_attn_W_dt, L0_attn_b_dt, L0_attn_A_log, L0_attn_D, L0_ffn_router_w, L0_ffn_gate_w, L0_ffn_up_w, L0_ffn_down_w, L0_ffn_shared_gate_w, L0_ffn_shared_up_w, L0_ffn_shared_down_w):

    def _L0_attn_ref(x, W_x, W_dt, b_dt, A_log, D):
        import jax, jax.numpy as jnp
        import numpy as np
        B, L, D_INNER, N_STATE, DT_RANK = (2, 128, 256, 16, 64)
        R = W_dt.shape[1]
        N = A_log.shape[1]
        x_proj = x @ W_x.T
        dt_x, Bm, Cm = jnp.split(x_proj, [R, R + N], axis=-1)
        dt = jax.nn.softplus(dt_x @ W_dt.T + b_dt)
        A = -jnp.exp(A_log)
        dA = jnp.exp(jnp.einsum('bld,dn->bldn', dt, A))
        dBx = jnp.einsum('bld,bln,bld->bldn', dt, Bm, x)

        def step(h, inp):
            dA_t, dBx_t, C_t = inp
            h = dA_t * h + dBx_t
            y_t = jnp.einsum('bdn,bn->bd', h, C_t)
            return (h, y_t)
        h0 = jnp.zeros((x.shape[0], x.shape[2], N), dtype=jnp.float32)
        _, ys = jax.lax.scan(step, h0, (dA.swapaxes(0, 1), dBx.swapaxes(0, 1), Cm.swapaxes(0, 1)))
        y = ys.swapaxes(0, 1) + x * D
        return y

    def _L0_ffn_ref(hidden_states, router_w, gate_w, up_w, down_w, shared_gate_w, shared_up_w, shared_down_w):
        import jax, jax.numpy as jnp
        import numpy as np
        SEQ, BS, D, F, E = (128, 2, 256, 256, 8)
        S, B, Dm = hidden_states.shape
        x = hidden_states.reshape(-1, Dm)
        logits = x @ router_w
        expert_idx = jnp.argmax(logits, axis=-1)
        score = jax.nn.sigmoid(jnp.max(logits, axis=-1))
        xs = x * score[:, None]
        n_experts = router_w.shape[1]
        out = jnp.zeros_like(x)
        for e in range(n_experts):
            m = (expert_idx == e)[:, None]
            xe = jnp.where(m, xs, 0.0)
            h = jax.nn.silu(xe @ gate_w[e]) * (xe @ up_w[e])
            out = out + jnp.where(m, h @ down_w[e], 0.0)
        shared = jax.nn.silu(x @ shared_gate_w) * (x @ shared_up_w) @ shared_down_w
        return (out + shared).reshape(S, B, Dm)
    x = L0_attn_x
    x = x + 0.5 * _L0_ffn_ref(_layernorm(x, axis=-1), L0_ffn_router_w, L0_ffn_gate_w, L0_ffn_up_w, L0_ffn_down_w, L0_ffn_shared_gate_w, L0_ffn_shared_up_w, L0_ffn_shared_down_w)
    x = x + _L0_attn_ref(_layernorm(x, axis=-1), L0_attn_W_x, L0_attn_W_dt, L0_attn_b_dt, L0_attn_A_log, L0_attn_D)
    x = x + 0.5 * _L0_ffn_ref(_layernorm(x, axis=-1), L0_ffn_router_w, L0_ffn_gate_w, L0_ffn_up_w, L0_ffn_down_w, L0_ffn_shared_gate_w, L0_ffn_shared_up_w, L0_ffn_shared_down_w)
    return x

_drawn_inputs = setup_inputs


def setup_inputs(seed=0):
    import zlib

    import numpy as np

    out = dict(_drawn_inputs(seed))
    spreads = {'L0_attn_D': (1.0, 0.2)}
    factors = {'L0_attn_W_x': 4.722,
     'L0_attn_W_dt': 8.0,
     'L0_attn_b_dt': 7.197,
     'L0_attn_A_log': 6.79,
     'L0_ffn_router_w': 8.0,
     'L0_ffn_gate_w': 8.0,
     'L0_ffn_up_w': 8.0,
     'L0_ffn_down_w': 8.0,
     'L0_ffn_shared_gate_w': 4.54,
     'L0_ffn_shared_up_w': 4.483,
     'L0_ffn_shared_down_w': 4.482}
    for name, (base, spread) in spreads.items():
        noise = np.random.default_rng([zlib.crc32(name.encode()), seed]).standard_normal(out[name].shape)
        drawn = base * np.exp(spread * noise) if base else spread * noise
        out[name] = jnp.asarray(drawn.astype(out[name].dtype))
    for name, factor in factors.items():
        out[name] = (out[name] * factor).astype(out[name].dtype)
    return out
```

```python
from contextlib import ExitStack

import concourse.bass as bass
from concourse import mybir

ALU = mybir.AluOpType
ACT = mybir.ActivationFunctionType
AX = mybir.AxisListType
F32 = mybir.dt.float32
BF16 = mybir.dt.bfloat16
I32 = mybir.dt.int32
U32 = mybir.dt.uint32

P = 128
LN_EPS = 1e-5


def macaron_kernel(nc, x, w_xT, w_dtT, b_dt, a_log, d_skip, router_w, gate_w, up_w, down_w,
                   sh_gate_w, sh_up_w, sh_down_w, out):
    BATCH, L, D = x.shape
    E, _, F = gate_w.shape
    R = w_dtT.shape[0]
    N = a_log.shape[1]
    KC = D // P
    LT = L // P
    GT = BATCH * LT
    TOK = GT * P
    RUNS = 2
    NR = GT + E - 1
    TS = NR + 2
    SHARED = E
    assert D == F == KC * P and L == 512 and GT == 16 and E == 8 and NR == 23 and N == 16

    x_rows = x.rearrange("b l d -> (b l) d").rearrange("(t p) d -> p t d", p=P)
    out_rows = out.rearrange("b l d -> (b l) d").rearrange("(t p) d -> p t d", p=P)
    sorted_rows = nc.dram_tensor("sorted_rows", [NR * P, D], F32, kind="Internal").ap()
    expert_out = nc.dram_tensor("expert_out", [NR * P, D], F32, kind="Internal").ap()

    with ExitStack() as ctx:
        def sb(name, shape, dt=F32):
            return ctx.enter_context(nc.sbuf_tensor(name, shape, dt))

        def sem(name):
            return ctx.enter_context(nc.semaphore(name))

        x_sb = sb("x_sb", [P, GT, D])
        xn = sb("xn", [P, GT, D])
        xnT = sb("xnT", [P, KC, TOK])
        w_gu = sb("w_gu", [P, KC, E + 1, 2 * F])
        w_dn = sb("w_dn", [P, KC, E + 1, D])
        w_rt = sb("w_rt", [P, KC, E])
        w_x = sb("w_x", [P, KC, R + 3 * 2 * N])
        w_dt = sb("w_dt", [R, D])
        b_sb = sb("b_sb", [P, KC])
        d_sb = sb("d_sb", [P, KC])
        a_in = sb("a_in", [P, KC, N])
        a_exp = sb("a_exp", [P, KC, N])
        a_neg = sb("a_neg", [P, KC, N])
        dt_sb = sb("dt_sb", [P, KC, TOK])
        dtx = sb("dtx", [P, KC, TOK])
        bc_parts = sb("bc_parts", [96, TOK], BF16)
        ident = sb("ident", [P, P])
        before = sb("before", [P, P], BF16)
        ones = sb("ones", [P, P], BF16)
        pick = sb("pick", [96, 2 * N], BF16)
        zero_row = sb("zero_row", [P, D])
        neg_half = sb("neg_half", [P, LT])
        e_less = sb("e_less", [P, E])
        tile_no = sb("tile_no", [P, NR])
        tile_first = sb("tile_first", [P, GT])
        keep = sb("keep", [P, E, GT])
        stats = sb("stats", [P, GT, 6])
        mv = sb("mv", [P, GT, 2])
        var_eps = sb("var_eps", [P, GT])
        rstd = sb("rstd", [P, GT])
        top = sb("top", [P, GT])
        is_top = sb("is_top", [P, GT, E])
        cand = sb("cand", [P, GT, E])
        first = sb("first", [P, GT])
        onehot = sb("onehot", [P, E, GT], BF16)
        score = sb("score", [P, 3, GT])
        upto = sb("upto", [P, E, GT])
        over = sb("over", [P, E, GT])
        n_tiles = sb("n_tiles", [P, E])
        tiles_upto = sb("tiles_upto", [P, E])
        ones_e = sb("ones_e", [P, E])
        start_e = sb("start_e", [P, 2, E])
        slot_m = sb("slot_m", [P, 4, E, GT])
        slot_f = sb("slot_f", [P, GT])
        slot = sb("slot", [P, GT], U32)
        past = sb("past", [P, NR, E])
        expert_f = sb("expert_f", [P, NR])
        expert = sb("expert", [P, NR], I32)
        xg = sb("xg", [P, 4, D])
        tt = sb("tt", [P, 2, 4, P])
        th = sb("th", [P, 2, F])
        q_sb = sb("q_sb", [P, 2, F])
        h_sb = sb("h_sb", [P, 2, F])
        y_sb = sb("y_sb", [P, 4, D])
        da = sb("da", [P, 2, KC, L])
        dbx = sb("dbx", [P, 2, KC, L])
        hs = sb("hs", [P, 2, KC, L])
        gs = sb("gs", [P, 2, KC, L])
        c_sb = sb("c_sb", [P, 2, L])
        sh_th = hs[:, 0]
        sh_q = hs[:, 1]
        sh_h = gs
        sp_exp = xg[:].rearrange("p a d -> p (a d)").rearrange("p (k t) -> p k t", k=KC)
        sp_ln = y_sb[:].rearrange("p a d -> p (a d)").rearrange("p (k t) -> p k t", k=KC)
        rank_sb = tt[0:R, 0].rearrange("p a t -> p (a t)")
        split_r = tt[:, 1].rearrange("p a t -> p (a t)")
        mid_part = th[:].rearrange("p a f -> p (a f)").bitcast(BF16)[:, 0:L]

        bank = [ctx.enter_context(nc.psum_tensor(f"bank{i}", [P, 512], F32)) for i in range(8)]
        H = bank[0:2]
        T, Y = bank[2], bank[3]
        PB = (bank[4], H[0])
        PC = (bank[5], H[1])
        YA = bank[6:8]
        YS = bank[4:6]
        LG = YS[0][:, 0:GT * E].rearrange("p (i e) -> p i e", e=E)
        RANK = YS[1][:, 0:E * GT].rearrange("p (e i) -> p e i", e=E)
        COUNT = YS[1][:, E * GT:2 * E * GT].rearrange("p (e i) -> p e i", e=E)

        x_in = [sem(f"x_in{b}") for b in range(BATCH)]
        small_in = sem("small_in")
        a_log_in = sem("a_log_in")
        router_in = sem("router_in")
        shared_in = sem("shared_in")
        experts_in = sem("experts_in")
        zeros_set = sem("zeros_set")
        zeros_out = sem("zeros_out")
        consts = sem("consts")
        pool_chain = sem("pool_chain")
        dve_chain = sem("dve_chain")
        ln_stats, ln_rstd, ln_xn, ln_tp, ln_xnT = (sem(f"ln_{s}") for s in ("stats", "rstd", "xn", "tp", "xnT"))
        rt_logits, rt_top, rt_exp, rt_onehot, rt_count, rt_read, rt_slot, rt_expert, rt_scaled, rt_scattered = (
            sem(f"rt_{s}") for s in ("logits", "top", "exp", "onehot", "count", "read", "slot", "expert", "scaled",
                                     "scattered"))
        sh_gu, sh_tanh, sh_mul, sh_hidden, sh_y, sh_x = (
            sem(f"sh_{s}") for s in ("gu", "tanh", "mul", "hidden", "y", "x"))
        ff_gu, ff_tanh, ff_mul, ff_hidden, ff_tp, ff_tpc, ff_y, ff_yc = (
            sem(f"ff_{s}") for s in ("gu", "tanh", "mul", "hidden", "tp", "tpc", "y", "yc"))
        ff_in = [sem(f"ff_in{u}") for u in range(4)]
        ff_out = [sem(f"ff_out{u}") for u in range(4)]
        back_in = [sem(f"back_in{i}") for i in range(GT)]
        back_x = sem("back_x")
        a_ready = sem("a_ready")
        pj_bc, pj_hi, pj_split, pj_rank, pj_rankc, pj_z, pj_abs, pj_exp, pj_w, pj_tmp, pj_ln, pj_max, pj_dt, pj_dtx, pj_xd = (
            sem(f"pj_{s}") for s in ("bc", "hi", "split", "rank", "rankc", "z", "abs", "exp", "w", "tmp", "ln", "max",
                                     "dt", "dtx", "xd"))
        sc_b, sc_c, sc_cc, sc_da, sc_dbx, sc_h, sc_g, sc_tp, sc_x = (
            sem(f"sc_{s}") for s in ("b", "c", "cc", "da", "dbx", "h", "g", "tp", "x"))
        done = sem("done")

        def pj_banks(b):
            return YA if b == 0 else (T, Y)

        block = ctx.enter_context(nc.Block())

        def uses(u):
            return len(range(u, NR, 4))

        @block.sync
        def _(sp):
            def rows_of(b):
                return slice(b * LT, (b + 1) * LT)

            for b in range(BATCH):
                sp.dma_start(x_sb[:, rows_of(b), :], x_rows[:, rows_of(b), :]).then_inc(x_in[b], 16)
                if b == 0:
                    sp.dma_start(w_rt[:], router_w.rearrange("(k p) e -> p k e", p=P)).then_inc(router_in, 16)
            sp.dma_start(w_gu[:, :, SHARED, 0:F], sh_gate_w.rearrange("(k p) f -> p k f", p=P)).then_inc(shared_in, 16)
            sp.dma_start(w_gu[:, :, SHARED, F:], sh_up_w.rearrange("(k p) f -> p k f", p=P)).then_inc(shared_in, 16)
            sp.dma_start(w_dn[:, :, SHARED, :], sh_down_w.rearrange("(k p) f -> p k f", p=P)).then_inc(shared_in, 16)
            sp.wait_ge(zeros_set, 1)
            sp.dma_start(sorted_rows.rearrange("(j p) d -> p j d", p=P),
                         zero_row[:].unsqueeze(1).to_broadcast([P, NR, D])).then_inc(zeros_out, 16)
            for k in range(KC):
                for w, lo in ((gate_w, 0), (up_w, F)):
                    sp.dma_start(w_gu[:, k, 0:E, lo:lo + F],
                                 w[:, k * P:(k + 1) * P, :].rearrange("e p f -> p e f")).then_inc(experts_in, 16)
                sp.dma_start(w_dn[:, k, 0:E, :],
                             down_w[:, k * P:(k + 1) * P, :].rearrange("e p f -> p e f")).then_inc(experts_in, 16)
            sp.dma_start(w_x[:, :, 0:R], w_xT[:, 0:R].rearrange("(k p) r -> p k r", p=P)).then_inc(small_in, 16)
            for c in range(3):
                sp.dma_start(w_x[:, :, R + c * 2 * N:R + (c + 1) * 2 * N],
                             w_xT[:, R:].rearrange("(k p) r -> p k r", p=P)).then_inc(small_in, 16)
            sp.dma_start(w_dt[:], w_dtT).then_inc(small_in, 16)
            sp.dma_start(b_sb[:], b_dt).then_inc(small_in, 16)
            sp.dma_start(d_sb[:], d_skip).then_inc(small_in, 16)
            sp.dma_start(a_in[:], a_log.rearrange("(k p) n -> p k n", p=P)).then_inc(a_log_in, 16)

            def load(r, j0, i4=0):
                u = j0 % 4
                if j0 >= 4:
                    sp.wait_ge(ff_tp, TS * r + j0 - 3 + i4)
                elif r > 0:
                    sp.wait_ge(ff_tp, TS * r)
                sp.dma_start(xg[:, u, :], sorted_rows[bass.ds((j0 + i4) * P, P), :]).then_inc(ff_in[u], 16)

            def store(r, j0, i4=0):
                sp.wait_ge(ff_yc, 1 + NR * r + j0 + 1 + i4)
                sp.dma_start(expert_out[bass.ds((j0 + i4) * P, P), :], y_sb[:, j0 % 4, :]).then_inc(ff_out[j0 % 4], 16)

            for r in range(RUNS):
                sp.wait_ge(rt_scattered, 16 * GT * (r + 1))
                for j in range(6):
                    load(r, j)
                with nc.Fori(0, NR - 10, 4, engines=[nc.sync.engine]) as i4:
                    for u in range(4):
                        load(r, 6 + u, i4)
                        store(r, u, i4)
                load(r, NR - 1)
                for j in range(NR - 7, NR):
                    store(r, j)
            for b in range(BATCH):
                sp.wait_ge(back_x, GT + LT * (b + 1))
                sp.dma_start(out_rows[:, rows_of(b), :], x_sb[:, rows_of(b), :]).then_inc(done, 16)
            sp.wait_ge(done, 16 * BATCH)

        @block.gpsimd
        def _(pool):
            chain = [0]

            def link(ins):
                chain[0] += 1
                ins.then_inc(pool_chain, 1)
                pool.wait_ge(pool_chain, chain[0])

            nc.gpsimd.memset(zero_row[:], 0.0).then_inc(zeros_set, 1)
            nc.gpsimd.memset(neg_half[:], -0.5)
            nc.gpsimd.memset(ident[:], 0.0)
            nc.gpsimd.memset(before[:], 1.0)
            nc.gpsimd.memset(ones[:], 1.0)
            nc.gpsimd.memset(ones_e[:], 1.0)
            nc.gpsimd.memset(keep[:], 1.0)
            nc.gpsimd.iota(e_less[:], [[1, E]], base=-E, channel_multiplier=0, allow_small_or_imprecise_dtypes=True)
            nc.gpsimd.iota(tile_no[:], [[1, NR]], base=0, channel_multiplier=0, allow_small_or_imprecise_dtypes=True)
            nc.gpsimd.iota(tile_first[:], [[P, GT]], base=0, channel_multiplier=0, allow_small_or_imprecise_dtypes=True)
            link(nc.gpsimd.memset(pick[:], 0.0))
            nc.gpsimd.affine_select(out=ident[:], in_=ident[:], compare_op=ALU.not_equal, fill=1.0, base=0,
                                    pattern=[[-1, P]], channel_multiplier=1)
            nc.gpsimd.affine_select(out=before[:], in_=before[:], compare_op=ALU.is_gt, fill=0.0, base=0,
                                    pattern=[[1, P]], channel_multiplier=-1)
            nc.gpsimd.memset(keep[:, :, 0:1], 0.0).then_inc(consts, 1)
            for c in range(3):
                pick_step = (nc.gpsimd.affine_select(out=pick[:], in_=pick[:], compare_op=ALU.not_equal, fill=1.0, base=-32 * c,
                                             pattern=[[-1, 2 * N]], channel_multiplier=1))
                if c < 2:
                    link(pick_step)
                else:
                    pick_step.then_inc(consts, 1)

            def rstd_of(c, b):
                tiles = slice(b * LT, (b + 1) * LT)
                pool.wait_ge(ln_stats, BATCH * c + b + 1)
                link(nc.gpsimd.tensor_scalar(var_eps[:, tiles], mv[:, tiles, 1], 1.0, LN_EPS, ALU.mult, ALU.add))
                nc.gpsimd.tensor_tensor(rstd[:, tiles], var_eps[:, tiles], neg_half[:], ALU.pow).then_inc(ln_rstd, 1)

            def scatter(r):
                pool.wait_ge(rt_slot, r + 1)
                if r == 0:
                    pool.wait_ge(zeros_out, 16)
                for i in range(GT):
                    if i % LT == 0:
                        pool.wait_ge(rt_scaled, BATCH * r + i // LT + 1)
                    nc.gpsimd.indirect_dma_start(
                        out=sorted_rows, out_offset=bass.IndirectOffsetOnAxis(ap=slot[:, i:i + 1], axis=0),
                        in_=xn[:, i, :], in_offset=None).then_inc(rt_scattered, 16)

            def gather(r):
                for u in range(4):
                    pool.wait_ge(ff_out[u], 16 * uses(u) * (r + 1))
                for i in range(GT):
                    nc.gpsimd.indirect_dma_start(
                        out=xn[:, i, :], out_offset=None, in_=expert_out,
                        in_offset=bass.IndirectOffsetOnAxis(ap=slot[:, i:i + 1], axis=0)).then_inc(back_in[i], 16)

            def scan(b):
                def step(n0, i2=0):
                    s = N * b + n0 + i2
                    pool.wait_ge(sc_h, KC * s + KC)
                    pool.wait_ge(sc_cc, s + 1)
                    if not (b == 0 and n0 < 2):
                        pool.wait_ge(sc_tp, s - 1)
                    u = n0 % 2
                    nc.gpsimd.tensor_tensor(gs[:, u], hs[:, u], c_sb[:, u].unsqueeze(1).to_broadcast([P, KC, L]),
                                            ALU.mult).then_inc(sc_g, 1)

                step(0)
                step(1)
                with nc.Fori(0, 5, 2, engines=[nc.gpsimd.engine]) as i2:
                    step(2, i2)
                    step(3, i2)
                if b > 0:
                    rstd_of(2, b - 1)
                with nc.Fori(0, 5, 2, engines=[nc.gpsimd.engine]) as i2:
                    step(8, i2)
                    step(9, i2)
                step(14)
                step(15)

            for b in range(BATCH):
                rstd_of(0, b)
            scatter(0)
            gather(0)
            for b in range(BATCH):
                rstd_of(1, b)
            for b in range(BATCH):
                scan(b)
            rstd_of(2, BATCH - 1)
            scatter(1)
            gather(1)

        @block.scalar
        def _(act):
            def ln_copies(c, b):
                for q in range(2 * b, 2 * b + 2):
                    act.wait_ge(ln_tp, (GT // 2) * c + q + 1)
                    src = (T, Y)[q % 2][:, :].rearrange("p (i k t) -> p i k t", i=2, k=KC)
                    dst = xnT[:, :, 2 * q * P:(2 * q + 2) * P].rearrange("p k (i t) -> p i k t", i=2)
                    nc.scalar.activation(dst, src, ACT.Copy).then_inc(ln_xnT, 1)

            def shared(r):
                for u in range(2 * BATCH * r, 2 * BATCH * (r + 1)):
                    act.wait_ge(sh_gu, u + 1)
                    if u >= 2:
                        act.wait_ge(sh_mul, u - 1)
                    nc.scalar.activation(sh_th[:, u % 2], (H[0], T)[u % 2][:, :], ACT.Tanh, scale=0.5).then_inc(sh_tanh, 1)

            def routed(r):
                def tanh(j0, i4=0):
                    act.wait_ge(ff_gu, NR * r + j0 + 1 + i4)
                    if r > 0 or j0 >= 2:
                        act.wait_ge(ff_mul, NR * r + j0 - 1 + i4)
                    nc.scalar.activation(th[:, j0 % 2], H[j0 % 2][:, 0:F], ACT.Tanh, scale=0.5).then_inc(ff_tanh, 1)

                def copy(j0, i4=0, lo=0, hi=4):
                    act.wait_ge(ff_tp, TS * r + j0 + 2 + i4)
                    nc.scalar.activation(tt[:, (j0 + 1) % 2, lo:hi], T[:, lo * P:hi * P].rearrange("p (a t) -> p a t", t=P),
                                         ACT.Copy).then_inc(ff_tpc, 1)

                copy(-1, lo=2)
                tanh(0)
                copy(0, lo=2)
                tanh(1)
                copy(1)
                with nc.Fori(0, NR - 6, 4, engines=[nc.scalar.engine]) as i4:
                    for j0 in range(2, 6):
                        tanh(j0, i4)
                        copy(j0, i4)
                tanh(NR - 1)
                copy(NR - 1, hi=2)
                copy(NR, hi=2)

            def route(r):
                act.wait_ge(rt_top, r + 1)
                nc.scalar.activation(score[:, 0], top[:], ACT.Exp, scale=-1.0).then_inc(rt_exp, 1)

            def project_bc(b):
                ts = slice(b * L, (b + 1) * L)
                act.wait_ge(pj_bc, b + 1)
                nc.scalar.activation(bc_parts[:, ts], pj_banks(b)[0][0:96, :], ACT.Copy).then_inc(pj_hi, 1)
                act.wait_ge(pj_rank, b + 1)
                nc.scalar.activation(rank_sb, pj_banks(b)[1][0:R, :], ACT.Copy).then_inc(pj_rankc, 1)

            def project_exp(b):
                for k in range(KC):
                    act.wait_ge(pj_z, KC * b + k + 1)
                    if b > 0:
                        act.wait_ge(pj_dt, b)
                    nc.scalar.activation(sp_exp[:, k], pj_banks(b)[k][:, :], ACT.Abs, bias=b_sb[:, k:k + 1]).then_inc(pj_abs, 1)
                act.wait_ge(pj_abs, KC * (b + 1))
                nc.scalar.activation(sp_exp, sp_exp, ACT.Exp, scale=-1.0).then_inc(pj_exp, 1)

            def project_ln(b):
                act.wait_ge(pj_tmp, b + 1)
                nc.scalar.activation(sp_ln, sp_ln, ACT.Ln).then_inc(pj_ln, 1)

            def scan(b):
                lo = b * L

                def step(n0, i2=0):
                    s = N * b + n0 + i2
                    u = n0 % 2
                    if not (b == 0 and n0 < 2):
                        act.wait_ge(sc_h, KC * (s - 1))
                    for k in range(KC):
                        nc.scalar.activation(da[:, u, k], dt_sb[:, k, lo:lo + L], ACT.Exp,
                                             scale=a_neg[:, k, bass.ds(n0 + i2, 1)]).then_inc(sc_da, 1)
                    act.wait_ge(sc_c, s + 1)
                    if not (b == 0 and n0 < 2):
                        act.wait_ge(sc_g, s - 1)
                    nc.scalar.activation(c_sb[:, u], PC[u][:, :], ACT.Copy).then_inc(sc_cc, 1)

                act.wait_ge(pj_dt, b + 1)
                step(0)
                step(1)
                with nc.Fori(0, 3, 2, engines=[nc.scalar.engine]) as i2:
                    step(2, i2)
                    step(3, i2)
                if b + 1 < BATCH:
                    project_bc(b + 1)
                with nc.Fori(0, 3, 2, engines=[nc.scalar.engine]) as i2:
                    step(6, i2)
                    step(7, i2)
                if b + 1 < BATCH:
                    project_exp(b + 1)
                with nc.Fori(0, 3, 2, engines=[nc.scalar.engine]) as i2:
                    step(10, i2)
                    step(11, i2)
                step(14)
                if b + 1 < BATCH:
                    project_ln(b + 1)
                step(15)

            for b in range(BATCH):
                ln_copies(0, b)
            route(0)
            shared(0)
            routed(0)
            act.wait_ge(a_log_in, 16)
            nc.scalar.activation(a_exp[:], a_in[:], ACT.Exp).then_inc(a_ready, 1)
            act.wait_ge(a_ready, 1)
            nc.scalar.activation(a_neg[:], a_exp[:], ACT.Copy, scale=-1.0).then_inc(a_ready, 1)
            ln_copies(1, 0)
            project_bc(0)
            ln_copies(1, 1)
            project_exp(0)
            ln_copies(1, 2)
            project_ln(0)
            ln_copies(1, 3)
            act.wait_ge(a_ready, 2)
            for b in range(BATCH):
                scan(b)
            for b in range(BATCH):
                ln_copies(2, b)
            route(1)
            shared(1)
            routed(1)

        @block.tensor
        def _(pe):
            def ln_transposes(c, b):
                for q in range(2 * b, 2 * b + 2):
                    pe.wait_ge(ln_xn, GT * c + 2 * q + 2)
                    if q >= 2:
                        pe.wait_ge(ln_xnT, (GT // 2) * c + q - 1)
                    dst = (T, Y)[q % 2]
                    for i in range(2):
                        for k in range(KC):
                            last = nc.tensor.transpose(dst[:, (i * KC + k) * P:(i * KC + k + 1) * P],
                                                       xn[:, 2 * q + i, k * P:(k + 1) * P], ident[:])
                    last.then_inc(ln_tp, 1)

            def route(r, b):
                c = 2 * r
                if r == 1 and b == 0:
                    pe.wait_ge(sc_dbx, N * BATCH)
                    pe.wait_ge(sc_cc, N * BATCH)
                pe.wait_ge(ln_xnT, (GT // 2) * c + 2 * b + 2)
                for i in range(LT * b, LT * (b + 1)):
                    for k in range(KC):
                        last = nc.tensor.matmul(LG[:, i, :], xnT[:, k, i * P:(i + 1) * P], w_rt[:, k, :],
                                                start=(k == 0), stop=(k == KC - 1))
                last.then_inc(rt_logits, 1)

            def count(r):
                pe.wait_ge(rt_onehot, r + 1)
                flat = onehot[:].rearrange("p e i -> p (e i)")
                nc.tensor.matmul(YS[1][:, 0:E * GT], before[:], flat, start=True, stop=True)
                nc.tensor.matmul(YS[1][:, E * GT:2 * E * GT], ones[:], flat, start=True, stop=True).then_inc(rt_count, 1)

            def shared(r):
                def gate_up(b, fo):
                    if b > 0:
                        pe.wait_ge(sh_hidden, 2 * (BATCH * r + b - 1) + fo + 1)
                    for w, dst in ((0, (H[0], T)[fo]), (F, (H[1], Y)[fo])):
                        for k in range(KC):
                            last = nc.tensor.matmul(dst[:, :], w_gu[:, k, SHARED, w + fo * P:w + (fo + 1) * P],
                                                    xnT[:, k, b * L:(b + 1) * L], start=(k == 0), stop=(k == KC - 1))
                    last.then_inc(sh_gu, 1)

                def down(b):
                    pe.wait_ge(sh_hidden, 2 * (BATCH * r + b + 1))
                    if b == 0:
                        pe.wait_ge(rt_read, r + 1)
                    for q in range(LT * b, LT * (b + 1)):
                        if q >= 2:
                            pe.wait_ge(sh_x, GT * r + q - 1)
                        for k in range(KC):
                            last = nc.tensor.matmul(YS[q % 2][:, 0:D], sh_h[:, b % 2, k, (q % LT) * P:(q % LT + 1) * P],
                                                    w_dn[:, k, SHARED, :], start=(k == 0), stop=(k == KC - 1))
                        last.then_inc(sh_y, 1)

                for b in range(BATCH):
                    gate_up(b, 0)
                    if b == 0:
                        count(r)
                    gate_up(b, 1)
                    if b > 0:
                        down(b - 1)
                down(BATCH - 1)

            def routed(r):

                def gate_up(j0, i4=0):
                    e = pe.value_load(expert[0:1, bass.ds(j0 + i4, 1)], min_val=0, max_val=E - 1)
                    pe.wait_ge(ff_tpc, TS * r + j0 + 1 + i4)
                    if j0 >= 2:
                        pe.wait_ge(ff_hidden, NR * r + j0 - 1 + i4)
                    for k in range(KC):
                        last = nc.tensor.matmul(H[j0 % 2][:, :], tt[:, j0 % 2, 2 + k], w_gu[:, k, bass.ds(e, 1), :].squeeze(1),
                                                start=(k == 0), stop=(k == KC - 1))
                    last.then_inc(ff_gu, 1)

                def turn(j0, i4=0):
                    if j0 >= 0:
                        pe.wait_ge(ff_tpc, TS * r + j0 + 1 + i4)
                    if j0 >= 1:
                        pe.wait_ge(ff_hidden, NR * r + j0 + i4)
                        for k in range(KC):
                            last = nc.tensor.transpose(T[:, k * P:(k + 1) * P], h_sb[:, (j0 - 1) % 2, k * P:(k + 1) * P], ident[:])
                    if j0 + 1 < NR:
                        u = (j0 + 1) % 4
                        pe.wait_ge(ff_in[u], 16 * (uses(u) * r + (j0 + 1) // 4 + 1) + 4 * i4)
                        for k in range(KC):
                            last = nc.tensor.transpose(T[:, (2 + k) * P:(3 + k) * P], xg[:, u, k * P:(k + 1) * P], ident[:])
                    last.then_inc(ff_tp, 1)

                def down(j0, i4=0):
                    e = pe.value_load(expert[0:1, bass.ds(j0 + i4, 1)], min_val=0, max_val=E - 1)
                    pe.wait_ge(ff_tpc, TS * r + j0 + 3 + i4)
                    pe.wait_ge(ff_yc, 1 + NR * r + j0 + i4)
                    for k in range(KC):
                        last = nc.tensor.matmul(Y[:, 0:D], tt[:, j0 % 2, k], w_dn[:, k, bass.ds(e, 1), :].squeeze(1),
                                                start=(k == 0), stop=(k == KC - 1))
                    last.then_inc(ff_y, 1)

                pe.wait_ge(rt_expert, r + 1)
                if r == 0:
                    pe.wait_ge(experts_in, 16 * 3 * KC)
                turn(-1)
                pe.wait_ge(sh_x, GT * (r + 1))
                gate_up(0)
                turn(0)
                gate_up(1)
                turn(1)
                with nc.Fori(0, NR - 6, 4, engines=[nc.tensor.engine]) as i4:
                    for j0 in range(2, 6):
                        gate_up(j0, i4)
                        turn(j0, i4)
                        down(j0 - 2, i4)
                gate_up(NR - 1)
                turn(NR - 1)
                down(NR - 3)
                turn(NR)
                down(NR - 2)
                down(NR - 1)

            def project_bc(b):
                lo = b * L
                pe.wait_ge(ln_xnT, GT // 2 + 2 * b + 2)
                if b == 1:
                    pe.wait_ge(ln_xnT, GT)
                if b > 1:
                    pe.wait_ge(pj_max, KC * b)
                for k in range(KC):
                    last = nc.tensor.matmul(pj_banks(b)[0][0:96, :], w_x[:, k, R:], xnT[:, k, lo:lo + L], start=(k == 0), stop=(k == KC - 1))
                last.then_inc(pj_bc, 1)

            def project_rank(b):
                lo = b * L
                for k in range(KC):
                    last = nc.tensor.matmul(pj_banks(b)[1][0:R, :], w_x[:, k, 0:R], xnT[:, k, lo:lo + L], start=(k == 0), stop=(k == KC - 1))
                last.then_inc(pj_rank, 1)

            def project_z(b):
                pe.wait_ge(pj_rankc, b + 1)
                pe.wait_ge(pj_split, b + 1)
                for k in range(KC):
                    nc.tensor.matmul(pj_banks(b)[k][:, :], w_dt[:, k * P:(k + 1) * P], rank_sb, start=True, stop=True).then_inc(pj_z, 1)

            def spread(b, n0, i2=0):
                s = N * b + n0 + i2
                u = n0 % 2
                if n0 + N * b == 0:
                    pe.wait_ge(pj_split, 1)
                if n0 == 0 and b > 0:
                    pe.wait_ge(pj_split, b + 1)
                for dst, m, used, signal in ((PB[u], 0, sc_dbx, sc_b), (PC[u], N, sc_cc, sc_c)):
                    if not (b == 0 and n0 < 2):
                        pe.wait_ge(used, s - 1)
                    nc.tensor.matmul(dst[:, :], pick[:, bass.ds(m + n0 + i2, 1)].to_broadcast([96, P]),
                                     bc_parts[:, b * L:(b + 1) * L], start=True, stop=True).then_inc(signal, 1)

            def scan(b):
                lo = b * L

                def add(n0, i2=0):
                    pe.wait_ge(sc_g, N * b + n0 + 1 + i2)
                    for k in range(KC):
                        for i in range(LT):
                            last = nc.tensor.matmul(YA[k][:, i * P:(i + 1) * P], gs[:, n0 % 2, k, i * P:(i + 1) * P], ident[:],
                                                    start=False, stop=(n0 == N - 1), is_transpose=True, skip_group_check=True)
                    last.then_inc(sc_tp, 1)

                def rounds(n0, count):
                    with nc.Fori(0, count - 1, 2, engines=[nc.tensor.engine]) as i2:
                        for u in range(2):
                            spread(b, n0 + u + 3, i2)
                            add(n0 + u, i2)

                if b > 0:
                    pe.wait_ge(sc_x, KC * b)
                pe.wait_ge(pj_xd, b + 1)
                for k in range(KC):
                    for i in range(LT):
                        nc.tensor.matmul(YA[k][:, i * P:(i + 1) * P], xnT[:, k, lo + i * P:lo + (i + 1) * P], ident[:],
                                         start=(i == 0), stop=False, is_transpose=True, skip_group_check=True)
                rounds(0, 4)
                if b + 1 < BATCH:
                    project_bc(b + 1)
                    project_rank(b + 1)
                rounds(4, 4)
                if b + 1 < BATCH:
                    project_z(b + 1)
                rounds(8, 4)
                spread(b, 15)
                add(12)
                for u in range(3):
                    if b + 1 < BATCH:
                        spread(b + 1, u)
                    add(13 + u)

            def normalised(c):
                for b in range(BATCH):
                    ln_transposes(c, b)
                    if b > 0 and c != 1:
                        route(c // 2, b - 1)
                if c != 1:
                    route(c // 2, BATCH - 1)

            pe.wait_ge(consts, 1)
            pe.wait_ge(router_in, 16)
            normalised(0)
            pe.wait_ge(shared_in, 16 * 3)
            shared(0)
            routed(0)
            pe.wait_ge(ff_yc, 1 + NR)
            pe.wait_ge(small_in, 16 * 7)
            ln_transposes(1, 0)
            project_bc(0)
            project_rank(0)
            ln_transposes(1, 1)
            project_z(0)
            for b in range(2, BATCH):
                ln_transposes(1, b)
            pe.wait_ge(consts, 2)
            for n in range(3):
                spread(0, n)
            for b in range(BATCH):
                scan(b)
            normalised(2)
            shared(1)
            routed(1)

        @block.vector
        def _(dve):
            chain = [0]

            def link(ins):
                chain[0] += 1
                ins.then_inc(dve_chain, 1)
                dve.wait_ge(dve_chain, chain[0])

            def stats_of(c, b):
                for i in range(LT * b, LT * (b + 1)):
                    last = nc.vector.bn_stats(stats[:, i], x_sb[:, i, :])
                link(last)
                for i in range(LT * b, LT * (b + 1)):
                    last = nc.vector.bn_aggr(mv[:, i], stats[:, i])
                last.then_inc(ln_stats, 1)

            def normalise(c, b):
                dve.wait_ge(ln_stats, BATCH * c + b + 1)
                dve.wait_ge(ln_rstd, BATCH * c + b + 1)
                for i in range(LT * b, LT * (b + 1)):
                    nc.vector.tensor_scalar(xn[:, i], x_sb[:, i, :], mv[:, i, 0:1], rstd[:, i:i + 1],
                                            ALU.subtract, ALU.mult).then_inc(ln_xn, 1)

            def route(r):
                dve.wait_ge(rt_logits, BATCH * (r + 1))
                nc.vector.tensor_reduce(top[:], LG, AX.X, ALU.max).then_inc(rt_top, 1)
                dve.wait_ge(rt_top, r + 1)
                link(nc.vector.tensor_tensor(is_top[:], LG, top[:].unsqueeze(2).to_broadcast([P, GT, E]), ALU.is_equal))
                e_row = e_less[:].unsqueeze(1).to_broadcast([P, GT, E])
                link(nc.vector.tensor_tensor(cand[:], is_top[:], e_row, ALU.mult))
                link(nc.vector.tensor_reduce(first[:], cand[:], AX.X, ALU.min))
                nc.vector.tensor_tensor(onehot[:], e_less[:].unsqueeze(2).to_broadcast([P, E, GT]),
                                        first[:].unsqueeze(1).to_broadcast([P, E, GT]), ALU.is_equal).then_inc(rt_onehot, 1)
                dve.wait_ge(rt_count, r + 1)
                flat = "p e i -> p (e i)"
                link(nc.vector.tensor_tensor_scan(upto[:].rearrange(flat), keep[:].rearrange(flat),
                                                  COUNT.rearrange(flat), 0.0, ALU.mult, ALU.add))
                nc.vector.tensor_tensor(slot_m[:, 0], upto[:], COUNT, ALU.subtract)
                link(nc.vector.tensor_tensor(over[:], upto[:, :, GT - 1:GT].to_broadcast([P, E, GT]),
                                             tile_first[:].unsqueeze(1).to_broadcast([P, E, GT]), ALU.is_gt))
                nc.vector.tensor_tensor(slot_m[:, 1], slot_m[:, 0], RANK, ALU.add).then_inc(rt_read, 1)
                link(nc.vector.tensor_reduce(n_tiles[:], over[:], AX.X, ALU.add))
                link(nc.vector.tensor_tensor_scan(tiles_upto[:], ones_e[:], n_tiles[:], 0.0, ALU.mult, ALU.add))
                link(nc.vector.tensor_tensor(start_e[:, 0], tiles_upto[:], n_tiles[:], ALU.subtract))
                link(nc.vector.tensor_scalar(start_e[:, 1], start_e[:, 0], float(P), None, ALU.mult))
                link(nc.vector.tensor_tensor(slot_m[:, 2], slot_m[:, 1], start_e[:, 1].unsqueeze(2).to_broadcast([P, E, GT]), ALU.add))
                link(nc.vector.tensor_tensor(slot_m[:, 3], slot_m[:, 2], onehot[:], ALU.mult))
                link(nc.vector.tensor_reduce(slot_f[:], slot_m[:, 3].rearrange("p e i -> p i e"), AX.X, ALU.add))
                nc.vector.tensor_copy(slot[:], slot_f[:]).then_inc(rt_slot, 1)
                dve.wait_ge(rt_exp, r + 1)
                link(nc.vector.tensor_scalar(score[:, 1], score[:, 0], 1.0, None, ALU.add))
                link(nc.vector.reciprocal(score[:, 2], score[:, 1]))
                dve.wait_ge(ln_tp, (GT // 2) * (2 * r + 1))
                for i in range(GT):
                    last = nc.vector.tensor_scalar(xn[:, i], xn[:, i], score[:, 2, i:i + 1], None, ALU.mult)
                    if i % LT == LT - 1:
                        last.then_inc(rt_scaled, 1)
                link(nc.vector.tensor_tensor(past[:], tiles_upto[:].unsqueeze(1).to_broadcast([P, NR, E]),
                                             tile_no[:].unsqueeze(2).to_broadcast([P, NR, E]), ALU.is_le))
                link(nc.vector.tensor_reduce(expert_f[:], past[:], AX.X, ALU.add))
                nc.vector.tensor_scalar(expert[:], expert_f[:], float(E - 1), None, ALU.min).then_inc(rt_expert, 1)

            def shared(r):
                for c2 in range(BATCH):
                    for fo in range(KC):
                        u = 2 * BATCH * r + 2 * c2 + fo
                        dve.wait_ge(sh_tanh, u + 1)
                        nc.vector.scalar_tensor_tensor(out=sh_q[:, fo], in0=sh_th[:, fo], scalar=1.0, in1=(H[0], T)[fo][:, :],
                                                       op0=ALU.add, op1=ALU.mult).then_inc(sh_mul, 1)
                        dve.wait_ge(sh_mul, u + 1)
                        nc.vector.tensor_tensor(sh_h[:, c2 % 2, fo], sh_q[:, fo], (H[1], Y)[fo][:, :], ALU.mult).then_inc(sh_hidden, 1)
                    for q in range(LT):
                        i = LT * c2 + q
                        dve.wait_ge(sh_y, GT * r + i + 1)
                        nc.vector.scalar_tensor_tensor(out=x_sb[:, i], in0=YS[q % 2][:, 0:D], scalar=0.25, in1=x_sb[:, i],
                                                       op0=ALU.mult, op1=ALU.add).then_inc(sh_x, 1)

            def routed(r):
                def hidden(j0, i4=0):
                    u = j0 % 2
                    dve.wait_ge(ff_tanh, NR * r + j0 + 1 + i4)
                    nc.vector.scalar_tensor_tensor(out=q_sb[:, u], in0=th[:, u], scalar=1.0, in1=H[u][:, 0:F],
                                                   op0=ALU.add, op1=ALU.mult).then_inc(ff_mul, 1)
                    dve.wait_ge(ff_mul, NR * r + j0 + 1 + i4)
                    if j0 >= 2:
                        dve.wait_ge(ff_tp, TS * r + j0 + 1 + i4)
                    nc.vector.tensor_tensor(h_sb[:, u], q_sb[:, u], H[u][:, F:], ALU.mult).then_inc(ff_hidden, 1)

                def result(j0, i4=0):
                    u = j0 % 4
                    dve.wait_ge(ff_y, NR * r + j0 + 1 + i4)
                    if r > 0 or j0 >= 4:
                        dve.wait_ge(ff_out[u], 16 * (uses(u) * r + j0 // 4) + 4 * i4)
                    nc.vector.tensor_copy(y_sb[:, u], Y[:, 0:D]).then_inc(ff_yc, 1)

                for j in range(6):
                    hidden(j)
                    if j >= 2:
                        result(j - 2)
                with nc.Fori(0, NR - 10, 4, engines=[nc.vector.engine]) as i4:
                    for j0 in range(6, 10):
                        hidden(j0, i4)
                        result(j0 - 2, i4)
                hidden(NR - 1)
                result(NR - 3)
                result(NR - 2)
                result(NR - 1)

            def combine(r, b):
                if b == 0:
                    dve.wait_ge(sh_x, GT * (r + 1))
                for i in range(LT * b, LT * (b + 1)):
                    dve.wait_ge(back_in[i], 16 * (r + 1))
                    nc.vector.scalar_tensor_tensor(out=x_sb[:, i], in0=xn[:, i], scalar=0.25, in1=x_sb[:, i],
                                                   op0=ALU.mult, op1=ALU.add).then_inc(back_x, 1)

            def project_split(b):
                ts = slice(b * L, (b + 1) * L)
                dve.wait_ge(pj_hi, b + 1)
                link(nc.vector.tensor_tensor(split_r[0:96], pj_banks(b)[0][0:96, :], bc_parts[:, ts], ALU.subtract))
                nc.vector.tensor_copy(bc_parts[32:64, ts], split_r[32:64])
                link(nc.vector.tensor_copy(mid_part[64:96], split_r[64:96]))
                nc.vector.tensor_tensor(bc_parts[64:96, ts], split_r[64:96], mid_part[64:96], ALU.subtract).then_inc(pj_split, 1)

            def project_w(b):
                ts = slice(b * L, (b + 1) * L)
                dve.wait_ge(pj_exp, b + 1)
                nc.vector.tensor_scalar(sp_ln, sp_exp, 1.0, None, ALU.add).then_inc(pj_w, 1)
                for k in range(KC):
                    nc.vector.tensor_scalar(dt_sb[:, k, ts], pj_banks(b)[k][:, :], b_sb[:, k:k + 1], 0.0, ALU.add, ALU.max).then_inc(pj_max, 1)
                dve.wait_ge(pj_w, b + 1)
                nc.vector.scalar_tensor_tensor(out=sp_exp, in0=sp_ln, scalar=-1.0, in1=sp_exp, op0=ALU.add, op1=ALU.subtract).then_inc(pj_tmp, 1)
                dve.wait_ge(pj_max, KC * (b + 1))
                dve.wait_ge(pj_tmp, b + 1)
                link(nc.vector.tensor_tensor(dt_sb[:, :, ts], dt_sb[:, :, ts], sp_exp, ALU.subtract))

            def project_dt(b):
                ts = slice(b * L, (b + 1) * L)
                dve.wait_ge(pj_ln, b + 1)
                nc.vector.tensor_tensor(dt_sb[:, :, ts], dt_sb[:, :, ts], sp_ln, ALU.add).then_inc(pj_dt, 1)
                dve.wait_ge(pj_dt, b + 1)
                nc.vector.tensor_tensor(dtx[:, :, ts], dt_sb[:, :, ts], xnT[:, :, ts], ALU.mult).then_inc(pj_dtx, 1)
                dve.wait_ge(pj_dtx, b + 1)
                for k in range(KC):
                    last = nc.vector.tensor_scalar(xnT[:, k, ts], xnT[:, k, ts], d_sb[:, k:k + 1], None, ALU.mult)
                last.then_inc(pj_xd, 1)

            def product(b, n0, i2=0):
                s = N * b + n0 + i2
                dve.wait_ge(sc_b, s + 1)
                if not (b == 0 and n0 < 2):
                    dve.wait_ge(sc_h, KC * (s - 1))
                nc.vector.tensor_tensor(dbx[:, n0 % 2], dtx[:, :, b * L:(b + 1) * L],
                                        PB[n0 % 2][:, :].unsqueeze(1).to_broadcast([P, KC, L]), ALU.mult).then_inc(sc_dbx, 1)

            def scan(b):
                def states(n0, i2=0):
                    s = N * b + n0 + i2
                    u = n0 % 2
                    for k in range(KC):
                        dve.wait_ge(sc_dbx, s + 1)
                        if not (b == 0 and n0 < 2):
                            dve.wait_ge(sc_g, s - 1)
                        dve.wait_ge(sc_da, KC * s + k + 1)
                        nc.vector.tensor_tensor_scan(hs[:, u, k], da[:, u, k], dbx[:, u, k], 0.0, ALU.mult, ALU.add).then_inc(sc_h, 1)
                        if k == 0:
                            if n0 < N - 1:
                                product(b, n0 + 1, i2)
                            elif b + 1 < BATCH:
                                product(b + 1, 0)

                def pairs(n0, count):
                    with nc.Fori(0, count - 1, 2, engines=[nc.vector.engine]) as i2:
                        states(n0, i2)
                        states(n0 + 1, i2)

                states(0)
                states(1)
                if b > 0:
                    add_y(b - 1)
                    dve.wait_ge(sc_x, KC * b)
                    stats_of(2, b - 1)
                pairs(2, 6)
                if b + 1 < BATCH:
                    project_split(b + 1)
                pairs(8, 2)
                if b > 0:
                    normalise(2, b - 1)
                pairs(10, 4)
                if b + 1 < BATCH:
                    project_w(b + 1)
                states(14)
                if b + 1 < BATCH:
                    project_dt(b + 1)
                states(15)

            def add_y(b):
                dve.wait_ge(sc_tp, N * (b + 1))
                for k in range(KC):
                    rows = x_sb[:, b * LT:(b + 1) * LT, k * P:(k + 1) * P]
                    nc.vector.tensor_tensor(rows, rows, YA[k][:, :].rearrange("p (i d) -> p i d", i=LT), ALU.add).then_inc(sc_x, 1)

            nc.vector.memset(first[:], 0.0).then_inc(ff_yc, 1)
            dve.wait_ge(consts, 1)
            for b in range(BATCH):
                dve.wait_ge(x_in[b], 16)
                stats_of(0, b)
                if b > 0:
                    normalise(0, b - 1)
            normalise(0, BATCH - 1)
            route(0)
            shared(0)
            routed(0)
            dve.wait_ge(small_in, 16 * 7)
            for b in range(BATCH):
                combine(0, b)
                dve.wait_ge(back_x, LT * (b + 1))
                stats_of(1, b)
                if b > 0:
                    normalise(1, b - 1)
                if b == 2:
                    project_split(0)
                if b == 3:
                    project_w(0)
            normalise(1, BATCH - 1)
            project_dt(0)
            product(0, 0)
            for b in range(BATCH):
                scan(b)
            add_y(BATCH - 1)
            dve.wait_ge(sc_x, KC * BATCH)
            stats_of(2, BATCH - 1)
            normalise(2, BATCH - 1)
            route(1)
            shared(1)
            routed(1)
            for b in range(BATCH):
                combine(1, b)


_NAMES = ['x', 'W_x', 'W_dt', 'b_dt', 'A_log', 'D', 'router_w', 'gate_w', 'up_w', 'down_w',
          'shared_gate_w', 'shared_up_w', 'shared_down_w']


def kernel(**inputs):
    import numpy as np
    import concourse.bacc as bacc
    from concourse.bass_utils import run_bass_kernel_spmd

    nc = bacc.Bacc("TRN2", target_bir_lowering=False, num_devices=1)
    arrays, args = {}, []
    for name in _NAMES:
        full = next(k for k in inputs if k in ("L0_attn_" + name, "L0_ffn_" + name))
        a = np.asarray(inputs[full])
        if name in ("W_x", "W_dt"):
            a = a.T
        if name in ("b_dt", "D"):
            a = a.reshape(-1, P).T
        a = np.ascontiguousarray(a)
        arrays["in_" + name] = a
        args.append(nc.dram_tensor("in_" + name, a.shape, mybir.dt.from_np(a.dtype), kind="ExternalInput").ap())
    shape = np.asarray(inputs["L0_attn_x"]).shape
    out = nc.dram_tensor("out", shape, F32, kind="ExternalOutput").ap()
    macaron_kernel(nc, *args, out)
    r = run_bass_kernel_spmd(nc, [arrays], core_ids=[0])
    return r.results[0]["out"]
```

```python
from contextlib import ExitStack

import concourse.bass as bass
from concourse import mybir

ALU = mybir.AluOpType
ACT = mybir.ActivationFunctionType
AX = mybir.AxisListType
F32 = mybir.dt.float32
BF16 = mybir.dt.bfloat16
I32 = mybir.dt.int32
U32 = mybir.dt.uint32

P = 128
LN_EPS = 1e-5


def macaron_kernel(nc, x, w_xT, w_dtT, b_dt, a_log, d_skip, router_w, gate_w, up_w, down_w,
                   sh_gate_w, sh_up_w, sh_down_w, out):
    BATCH, L, D = x.shape
    E, _, F = gate_w.shape
    R = w_dtT.shape[0]
    N = a_log.shape[1]
    KC = D // P
    LT = L // P
    GT = BATCH * LT
    TOK = GT * P
    RUNS = 2
    NR = GT + E - 1
    TS = NR + 2
    AHEAD = 2
    RING = 4
    SHARED = E
    assert D == F == KC * P and L == 512 and GT == 16 and E == 8 and NR == 23 and N == 16

    x_rows = x.rearrange("b l d -> (b l) d").rearrange("(t p) d -> p t d", p=P)
    out_rows = out.rearrange("b l d -> (b l) d").rearrange("(t p) d -> p t d", p=P)
    sorted_rows = [nc.dram_tensor(f"sorted_rows{r}", [NR * P, D + 1], F32, kind="Internal").ap() for r in range(RUNS)]
    sorted_tiles = [rows.rearrange("(j p) d -> p j d", p=P) for rows in sorted_rows]
    token_out = nc.dram_tensor("token_out", [TOK + NR * P, D], F32, kind="Internal").ap()
    token_out_tiles = token_out[0:TOK, :].rearrange("(t p) d -> p t d", p=P)

    with ExitStack() as ctx:
        def sb(name, shape, dt=F32):
            return ctx.enter_context(nc.sbuf_tensor(name, shape, dt))

        def sem(name):
            return ctx.enter_context(nc.semaphore(name))

        x_sb = sb("x_sb", [P, GT, D])
        xn_no = sb("xn_no", [P, GT, D + 1])
        xnT = sb("xnT", [P, KC, TOK])
        w_gu = sb("w_gu", [P, KC, E + 1, 2 * F])
        w_dn = sb("w_dn", [P, KC, E + 1, D])
        w_rt = sb("w_rt", [P, KC, E])
        w_x = sb("w_x", [P, KC, R + 3 * 2 * N])
        w_dt = sb("w_dt", [R, D])
        b_sb = sb("b_sb", [P, KC])
        d_sb = sb("d_sb", [P, KC])
        a_in = sb("a_in", [P, KC, N])
        a_exp = sb("a_exp", [P, KC, N])
        a_neg = sb("a_neg", [P, KC, N])
        dt_sb = sb("dt_sb", [P, KC, 2 * L])
        dtx = sb("dtx", [P, KC, 2 * L])
        bc_parts = sb("bc_parts", [96, TOK], BF16)
        ident = sb("ident", [P, P])
        before = sb("before", [P, P], BF16)
        ones = sb("ones", [P, P], BF16)
        pick = sb("pick", [96, 2 * N], BF16)
        zero_row = sb("zero_row", [P, D])
        neg_half = sb("neg_half", [P, LT])
        e_less = sb("e_less", [P, E])
        tile_no = sb("tile_no", [P, NR])
        tile_first = sb("tile_first", [P, GT])
        keep = sb("keep", [P, E, GT])
        stats = sb("stats", [P, GT, 6])
        mv = sb("mv", [P, GT, 2])
        var_eps = sb("var_eps", [P, GT])
        rstd = sb("rstd", [P, GT])
        top = sb("top", [P, GT])
        is_top = sb("is_top", [P, GT, E])
        cand = sb("cand", [P, GT, E])
        first = sb("first", [P, GT])
        onehot = sb("onehot", [P, E, GT], BF16)
        score = sb("score", [P, 3, GT])
        upto = sb("upto", [P, E, GT])
        over = sb("over", [P, E, GT])
        n_tiles = sb("n_tiles", [P, E])
        tiles_upto = sb("tiles_upto", [P, E])
        ones_e = sb("ones_e", [P, E])
        start_e = sb("start_e", [P, 2, E])
        slot_m = sb("slot_m", [P, 4, E, GT])
        slot_f = sb("slot_f", [P, GT])
        slot = sb("slot", [P, GT], U32)
        pad_no = sb("pad_no", [P, NR], U32)
        row_token = sb("row_token", [P, NR], U32)
        past = slot_m[:, 0:2].rearrange("p c e i -> p (c e i)")[:, 0:NR * E].rearrange("p (j e) -> p j e", e=E)
        expert_f = sb("expert_f", [P, NR])
        expert = sb("expert", [P, NR], I32)
        xg = sb("xg", [P, 4, D])
        tt = sb("tt", [P, 2, 4, P])
        th = sb("th", [P, 2, F])
        q_sb = sb("q_sb", [P, 2, F])
        h_sb = sb("h_sb", [P, 2, F])
        y_sb = sb("y_sb", [P, 4, D])
        da = sb("da", [P, RING, KC, L])
        hs = sb("hs", [P, RING, KC, L])
        dbx = sb("dbx", [P, 2, KC, L])
        gs = sb("gs", [P, 2, KC, L])
        c_sb = sb("c_sb", [P, RING, L])
        xn = xn_no[:, :, 0:D]
        sh_th = hs[:, 0]
        sh_q = hs[:, 1]
        sh_h = gs
        sp_exp = xg[:].rearrange("p a d -> p (a d)").rearrange("p (k t) -> p k t", k=KC)
        sp_ln = y_sb[:].rearrange("p a d -> p (a d)").rearrange("p (k t) -> p k t", k=KC)
        rank_sb = tt[0:R, 0].rearrange("p a t -> p (a t)")
        split_r = tt[:, 1].rearrange("p a t -> p (a t)")
        mid_part = th[:].rearrange("p a f -> p (a f)").bitcast(BF16)[:, 0:L]

        bank = [ctx.enter_context(nc.psum_tensor(f"bank{i}", [P, 512], F32)) for i in range(8)]
        H = bank[0:2]
        T, Y = bank[2], bank[3]
        PB = (bank[4], H[0])
        PC = (bank[5], H[1])
        YA = bank[6:8]
        YS = bank[4:6]
        LG = YS[0][:, 0:GT * E].rearrange("p (i e) -> p i e", e=E)
        RANK = YS[1][:, 0:E * GT].rearrange("p (e i) -> p e i", e=E)
        COUNT = YS[1][:, E * GT:2 * E * GT].rearrange("p (e i) -> p e i", e=E)

        x_in = [sem(f"x_in{b}") for b in range(BATCH)]
        small_in = sem("small_in")
        a_log_in = sem("a_log_in")
        router_in = sem("router_in")
        shared_in = sem("shared_in")
        experts_in = sem("experts_in")
        zeros_set = sem("zeros_set")
        zeros_out = sem("zeros_out")
        consts = sem("consts")
        pool_chain = sem("pool_chain")
        dve_chain = sem("dve_chain")
        ln_stats, ln_rstd, ln_xn, ln_tp, ln_xnT = (sem(f"ln_{s}") for s in ("stats", "rstd", "xn", "tp", "xnT"))
        rt_logits, rt_top, rt_exp, rt_onehot, rt_count, rt_read, rt_slot, rt_expert, rt_scaled, rt_scattered = (
            sem(f"rt_{s}") for s in ("logits", "top", "exp", "onehot", "count", "read", "slot", "expert", "scaled",
                                     "scattered"))
        sh_gu, sh_tanh, sh_mul, sh_hidden, sh_y, sh_x = (
            sem(f"sh_{s}") for s in ("gu", "tanh", "mul", "hidden", "y", "x"))
        ff_gu, ff_tanh, ff_mul, ff_hidden, ff_tp, ff_tpc, ff_y, ff_yc = (
            sem(f"ff_{s}") for s in ("gu", "tanh", "mul", "hidden", "tp", "tpc", "y", "yc"))
        ff_in = [sem(f"ff_in{u}") for u in range(4)]
        ff_out = [sem(f"ff_out{u}") for u in range(4)]
        ids_set = sem("ids_set")
        ids_in = sem("ids_in")
        back_in = [sem(f"back_in{b}") for b in range(BATCH)]
        back_x = sem("back_x")
        a_ready = sem("a_ready")
        pj_bc, pj_hi, pj_split, pj_rank, pj_rankc, pj_z, pj_abs, pj_exp, pj_w, pj_tmp, pj_corr, pj_ln, pj_max, pj_dt, pj_dtx, pj_xd = (
            sem(f"pj_{s}") for s in ("bc", "hi", "split", "rank", "rankc", "z", "abs", "exp", "w", "tmp", "corr", "ln", "max",
                                     "dt", "dtx", "xd"))
        sc_b, sc_c, sc_cc, sc_da, sc_dbx, sc_h, sc_g, sc_tp, sc_x = (
            sem(f"sc_{s}") for s in ("b", "c", "cc", "da", "dbx", "h", "g", "tp", "x"))
        sc_last = sem("sc_last")
        done = sem("done")

        def pj_banks(b):
            return YA if b == 0 else (T, Y)

        def ring(buffer, n0, i2):
            if isinstance(i2, int):
                return buffer[:, (n0 + i2) % RING]
            base = n0 % RING
            return buffer[:, bass.ds(i2 + base if base < 2 else base - i2, 1)].squeeze(1)

        def by_dve(b, n0):
            return b == BATCH - 1 and n0 >= N - 2

        def seq(b):
            return slice((b % 2) * L, (b % 2 + 1) * L)

        block = ctx.enter_context(nc.Block())

        def uses(u):
            return len(range(u, NR, 4))

        @block.sync
        def _(sp):
            def rows_of(b):
                return slice(b * LT, (b + 1) * LT)

            for b in range(BATCH):
                sp.dma_start(x_sb[:, rows_of(b), :], x_rows[:, rows_of(b), :]).then_inc(x_in[b], 16)
                if b == 0:
                    sp.dma_start(w_rt[:], router_w.rearrange("(k p) e -> p k e", p=P)).then_inc(router_in, 16)
            sp.dma_start(w_gu[:, :, SHARED, 0:F], sh_gate_w.rearrange("(k p) f -> p k f", p=P)).then_inc(shared_in, 16)
            sp.dma_start(w_gu[:, :, SHARED, F:], sh_up_w.rearrange("(k p) f -> p k f", p=P)).then_inc(shared_in, 16)
            sp.dma_start(w_dn[:, :, SHARED, :], sh_down_w.rearrange("(k p) f -> p k f", p=P)).then_inc(shared_in, 16)
            def fill(r):
                sp.dma_start(sorted_tiles[r][:, :, 0:D], zero_row[:].unsqueeze(1).to_broadcast([P, NR, D])).then_inc(zeros_out, 16)
                sp.dma_start(sorted_tiles[r][:, :, D], pad_no[:].bitcast(F32), allow_slow_non_contiguous=True).then_inc(zeros_out, 16)

            sp.wait_ge(zeros_set, 1)
            sp.wait_ge(ids_set, 1)
            fill(0)
            for k in range(KC):
                for w, lo in ((gate_w, 0), (up_w, F)):
                    sp.dma_start(w_gu[:, k, 0:E, lo:lo + F],
                                 w[:, k * P:(k + 1) * P, :].rearrange("e p f -> p e f")).then_inc(experts_in, 16)
                sp.dma_start(w_dn[:, k, 0:E, :],
                             down_w[:, k * P:(k + 1) * P, :].rearrange("e p f -> p e f")).then_inc(experts_in, 16)
            sp.dma_start(w_x[:, :, 0:R], w_xT[:, 0:R].rearrange("(k p) r -> p k r", p=P)).then_inc(small_in, 16)
            for c in range(3):
                sp.dma_start(w_x[:, :, R + c * 2 * N:R + (c + 1) * 2 * N],
                             w_xT[:, R:].rearrange("(k p) r -> p k r", p=P)).then_inc(small_in, 16)
            sp.dma_start(w_dt[:], w_dtT).then_inc(small_in, 16)
            sp.dma_start(b_sb[:], b_dt).then_inc(small_in, 16)
            sp.dma_start(d_sb[:], d_skip).then_inc(small_in, 16)
            sp.dma_start(a_in[:], a_log.rearrange("(k p) n -> p k n", p=P)).then_inc(a_log_in, 16)

            def load(r, j0, i4=0):
                u = j0 % 4
                if j0 >= 4:
                    sp.wait_ge(ff_tp, TS * r + j0 - 3 + i4)
                elif r > 0:
                    sp.wait_ge(ff_tp, TS * r)
                sp.dma_start(xg[:, u, :], sorted_rows[r][bass.ds((j0 + i4) * P, P), 0:D]).then_inc(ff_in[u], 16)

            for r in range(RUNS):
                sp.wait_ge(rt_scattered, 16 * GT * (r + 1))
                for j in range(4):
                    load(r, j)
                sp.dma_start(row_token[:].bitcast(F32), sorted_tiles[r][:, :, D], allow_slow_non_contiguous=True).then_inc(ids_in, 16)
                for j in range(4, 7):
                    load(r, j)
                with nc.Fori(0, NR - 10, 4, engines=[nc.sync.engine]) as i4:
                    for j0 in range(7, 11):
                        load(r, j0, i4)
                if r == 0:
                    fill(1)
                for u in range(4):
                    sp.wait_ge(ff_out[u], 16 * uses(u) * (r + 1))
                for b in range(BATCH):
                    sp.dma_start(xn[:, rows_of(b), :], token_out_tiles[:, rows_of(b), :]).then_inc(back_in[b], 16)
            for b in range(BATCH):
                sp.wait_ge(back_x, GT + LT * (b + 1))
                sp.dma_start(out_rows[:, rows_of(b), :], x_sb[:, rows_of(b), :]).then_inc(done, 16)
            sp.wait_ge(done, 16 * BATCH)

        @block.gpsimd
        def _(pool):
            chain = [0]

            def link(ins):
                chain[0] += 1
                ins.then_inc(pool_chain, 1)
                pool.wait_ge(pool_chain, chain[0])

            nc.gpsimd.memset(zero_row[:], 0.0).then_inc(zeros_set, 1)
            nc.gpsimd.iota(pad_no[:], [[P, NR]], base=TOK, channel_multiplier=1).then_inc(ids_set, 1)
            nc.gpsimd.iota(xn_no[:, :, D].bitcast(U32), [[P, GT]], base=0, channel_multiplier=1).then_inc(ids_set, 1)
            nc.gpsimd.memset(neg_half[:], -0.5)
            nc.gpsimd.memset(ident[:], 0.0)
            nc.gpsimd.memset(before[:], 1.0)
            nc.gpsimd.memset(ones[:], 1.0)
            nc.gpsimd.memset(ones_e[:], 1.0)
            nc.gpsimd.memset(keep[:], 1.0)
            nc.gpsimd.iota(e_less[:], [[1, E]], base=-E, channel_multiplier=0, allow_small_or_imprecise_dtypes=True)
            nc.gpsimd.iota(tile_no[:], [[1, NR]], base=0, channel_multiplier=0, allow_small_or_imprecise_dtypes=True)
            nc.gpsimd.iota(tile_first[:], [[P, GT]], base=0, channel_multiplier=0, allow_small_or_imprecise_dtypes=True)
            link(nc.gpsimd.memset(pick[:], 0.0))
            nc.gpsimd.affine_select(out=ident[:], in_=ident[:], compare_op=ALU.not_equal, fill=1.0, base=0,
                                    pattern=[[-1, P]], channel_multiplier=1)
            nc.gpsimd.affine_select(out=before[:], in_=before[:], compare_op=ALU.is_gt, fill=0.0, base=0,
                                    pattern=[[1, P]], channel_multiplier=-1)
            nc.gpsimd.memset(keep[:, :, 0:1], 0.0).then_inc(consts, 1)
            for c in range(3):
                pick_step = (nc.gpsimd.affine_select(out=pick[:], in_=pick[:], compare_op=ALU.not_equal, fill=1.0, base=-32 * c,
                                             pattern=[[-1, 2 * N]], channel_multiplier=1))
                if c < 2:
                    link(pick_step)
                else:
                    pick_step.then_inc(consts, 1)

            def rstd_of(c, b):
                tiles = slice(b * LT, (b + 1) * LT)
                pool.wait_ge(ln_stats, BATCH * c + b + 1)
                link(nc.gpsimd.tensor_scalar(var_eps[:, tiles], mv[:, tiles, 1], 1.0, LN_EPS, ALU.mult, ALU.add))
                nc.gpsimd.tensor_tensor(rstd[:, tiles], var_eps[:, tiles], neg_half[:], ALU.pow).then_inc(ln_rstd, 1)

            def project_corr(b, piece):
                corr = dtx[:, :, seq(b)]
                if piece == 0:
                    pool.wait_ge(pj_w, b + 1)
                    nc.gpsimd.tensor_scalar(corr, sp_ln, 1.0, -1.0, ALU.mult, ALU.add).then_inc(pj_tmp, 1)
                elif piece == 1:
                    pool.wait_ge(pj_tmp, b + 1)
                    nc.gpsimd.tensor_tensor(corr, corr, sp_exp, ALU.subtract).then_inc(pj_corr, 1)
                else:
                    pool.wait_ge(pj_max, KC * (b + 1))
                    pool.wait_ge(pj_corr, 2 * b - 1)
                    nc.gpsimd.tensor_tensor(dt_sb[:, :, seq(b)], dt_sb[:, :, seq(b)], corr, ALU.subtract).then_inc(pj_corr, 1)

            def scatter(r):
                pool.wait_ge(rt_slot, r + 1)
                if r == 0:
                    pool.wait_ge(ids_set, 2)
                pool.wait_ge(zeros_out, 32 * (r + 1))
                for i in range(GT):
                    if i % LT == 0:
                        pool.wait_ge(rt_scaled, BATCH * r + i // LT + 1)
                    nc.gpsimd.indirect_dma_start(
                        out=sorted_rows[r], out_offset=bass.IndirectOffsetOnAxis(ap=slot[:, i:i + 1], axis=0),
                        in_=xn_no[:, i, :], in_offset=None).then_inc(rt_scattered, 16)

            def scatter_back(r):
                pool.wait_ge(ids_in, 16 * (r + 1))
                if r > 0:
                    for b in range(BATCH):
                        pool.wait_ge(back_in[b], 16 * r)
                for j in range(NR):
                    pool.wait_ge(ff_yc, 1 + NR * r + j + 1)
                    nc.gpsimd.indirect_dma_start(
                        out=token_out, out_offset=bass.IndirectOffsetOnAxis(ap=row_token[:, j:j + 1], axis=0),
                        in_=y_sb[:, j % 4, :], in_offset=None).then_inc(ff_out[j % 4], 16)

            def scan(b):
                def step(n0, i2=0):
                    s = N * b + n0 + i2
                    pool.wait_ge(sc_h, KC * s + KC)
                    pool.wait_ge(sc_cc, s + 1)
                    if not (b == 0 and n0 < 2):
                        pool.wait_ge(sc_tp, s - 1)
                    nc.gpsimd.tensor_tensor(gs[:, n0 % 2], ring(hs, n0, i2), ring(c_sb, n0, i2).unsqueeze(1).to_broadcast([P, KC, L]),
                                            ALU.mult).then_inc(sc_g, 1)

                step(0)
                step(1)
                step(2)
                if b > 0:
                    rstd_of(2, b - 1)
                step(3)
                with nc.Fori(0, RING - 1, 2, engines=[nc.gpsimd.engine]) as i2:
                    step(4, i2)
                    step(5, i2)
                for piece in range(3):
                    step(8 + piece)
                    if b + 1 < BATCH:
                        project_corr(b + 1, piece)
                step(11)
                for n0 in range(12, N):
                    if not by_dve(b, n0):
                        step(n0)

            for b in range(BATCH):
                rstd_of(0, b)
            scatter(0)
            scatter_back(0)
            for b in range(BATCH):
                rstd_of(1, b)
            for b in range(BATCH):
                scan(b)
            rstd_of(2, BATCH - 1)
            scatter(1)
            scatter_back(1)

        @block.scalar
        def _(act):
            def ln_copy(c, q):
                act.wait_ge(ln_tp, (GT // 2) * c + q + 1)
                src = (T, Y)[q % 2][:, :].rearrange("p (i k t) -> p i k t", i=2, k=KC)
                dst = xnT[:, :, 2 * q * P:(2 * q + 2) * P].rearrange("p k (i t) -> p i k t", i=2)
                nc.scalar.activation(dst, src, ACT.Copy).then_inc(ln_xnT, 1)

            def ln_copies(c, b):
                for q in range(2 * b, 2 * b + 2):
                    ln_copy(c, q)

            def shared(r):
                for u in range(2 * BATCH * r, 2 * BATCH * (r + 1)):
                    act.wait_ge(sh_gu, u + 1)
                    if u >= 2:
                        act.wait_ge(sh_mul, u - 1)
                    nc.scalar.activation(sh_th[:, u % 2], (H[0], T)[u % 2][:, :], ACT.Tanh, scale=0.5).then_inc(sh_tanh, 1)

            def routed(r):
                def tanh(j0, i4=0):
                    act.wait_ge(ff_gu, NR * r + j0 + 1 + i4)
                    if r > 0 or j0 >= 2:
                        act.wait_ge(ff_mul, NR * r + j0 - 1 + i4)
                    nc.scalar.activation(th[:, j0 % 2], H[j0 % 2][:, 0:F], ACT.Tanh, scale=0.5).then_inc(ff_tanh, 1)

                def copy(j0, i4=0, lo=0, hi=4):
                    act.wait_ge(ff_tp, TS * r + j0 + 2 + i4)
                    nc.scalar.activation(tt[:, (j0 + 1) % 2, lo:hi], T[:, lo * P:hi * P].rearrange("p (a t) -> p a t", t=P),
                                         ACT.Copy).then_inc(ff_tpc, 1)

                copy(-1, lo=2)
                tanh(0)
                copy(0, lo=2)
                tanh(1)
                copy(1)
                with nc.Fori(0, NR - 6, 4, engines=[nc.scalar.engine]) as i4:
                    for j0 in range(2, 6):
                        tanh(j0, i4)
                        copy(j0, i4)
                tanh(NR - 1)
                copy(NR - 1, hi=2)
                copy(NR, hi=2)

            def route(r):
                act.wait_ge(rt_top, r + 1)
                nc.scalar.activation(score[:, 0], top[:], ACT.Exp, scale=-1.0).then_inc(rt_exp, 1)

            def project_bc(b):
                ts = slice(b * L, (b + 1) * L)
                act.wait_ge(pj_bc, b + 1)
                nc.scalar.activation(bc_parts[:, ts], pj_banks(b)[0][0:96, :], ACT.Copy).then_inc(pj_hi, 1)

            def project_rank(b):
                act.wait_ge(pj_rank, b + 1)
                nc.scalar.activation(rank_sb, pj_banks(b)[1][0:R, :], ACT.Copy).then_inc(pj_rankc, 1)

            def project_abs(b, k):
                act.wait_ge(pj_z, KC * b + k + 1)
                if b > 0:
                    act.wait_ge(pj_dt, b)
                nc.scalar.activation(sp_exp[:, k], pj_banks(b)[k][:, :], ACT.Abs, bias=b_sb[:, k:k + 1]).then_inc(pj_abs, 1)

            def project_max(b, k):
                nc.scalar.activation(dt_sb[:, k, seq(b)], pj_banks(b)[k][:, :], ACT.Relu, bias=b_sb[:, k:k + 1]).then_inc(pj_max, 1)

            def project_xd(b):
                act.wait_ge(pj_dtx, b + 1)
                for k in range(KC):
                    nc.scalar.activation(xnT[:, k, b * L:(b + 1) * L], xnT[:, k, b * L:(b + 1) * L], ACT.Copy,
                                         scale=d_sb[:, k:k + 1]).then_inc(pj_xd, 1)

            def project_exp(b, k):
                act.wait_ge(pj_abs, KC * b + k + 1)
                nc.scalar.activation(sp_exp[:, k], sp_exp[:, k], ACT.Exp, scale=-1.0).then_inc(pj_exp, 1)

            def project_ln(b, k):
                act.wait_ge(pj_tmp, b + 1)
                nc.scalar.activation(sp_ln[:, k], sp_ln[:, k], ACT.Ln).then_inc(pj_ln, 1)

            def scan(b):
                def decay(n0, i2=0):
                    s = N * b + n0 + i2
                    if not (b == 0 and n0 < RING):
                        act.wait_ge(sc_h, KC * (s - RING + 1))
                    for k in range(KC):
                        nc.scalar.activation(ring(da, n0, i2)[:, k], dt_sb[:, k, seq(b)], ACT.Exp,
                                             scale=a_neg[:, k, bass.ds(n0 + i2, 1)]).then_inc(sc_da, 1)

                def copy_c(n0, i2=0):
                    s = N * b + n0 + i2
                    act.wait_ge(sc_c, s + 1)
                    if not (b == 0 and n0 < RING):
                        act.wait_ge(sc_g, s - RING + 1)
                    nc.scalar.activation(ring(c_sb, n0, i2), PC[n0 % 2][:, :], ACT.Copy).then_inc(sc_cc, 1)

                def step(n0, i2=0):
                    copy_c(n0, i2)
                    if n0 + AHEAD < N:
                        decay(n0 + AHEAD, i2)

                more = b + 1 < BATCH
                act.wait_ge(pj_dt, b + 1)
                for n0 in range(AHEAD):
                    decay(n0)
                project_xd(b)
                step(0)
                step(1)
                loops = () if more else (2, 6)
                for n0 in range(2, N):
                    if n0 in loops:
                        with nc.Fori(0, RING - 1, 2, engines=[nc.scalar.engine]) as i2:
                            step(n0, i2)
                            step(n0 + 1, i2)
                        continue
                    if any(m < n0 < m + RING for m in loops):
                        continue
                    step(n0)
                    if more and n0 == 3:
                        project_bc(b + 1)
                    if more and n0 == 4:
                        project_rank(b + 1)
                    if more and n0 in (6, 7):
                        project_abs(b + 1, n0 - 6)
                        project_max(b + 1, n0 - 6)
                    if more and n0 == 8:
                        project_exp(b + 1, 0)
                        project_exp(b + 1, 1)
                    if more and n0 == 11:
                        project_ln(b + 1, 0)
                        project_ln(b + 1, 1)
                    if b > 0 and n0 in (13, 14):
                        ln_copy(2, 2 * (b - 1) + n0 - 13)

            for b in range(BATCH):
                ln_copies(0, b)
            route(0)
            shared(0)
            routed(0)
            act.wait_ge(a_log_in, 16)
            nc.scalar.activation(a_exp[:], a_in[:], ACT.Exp).then_inc(a_ready, 1)
            act.wait_ge(a_ready, 1)
            nc.scalar.activation(a_neg[:], a_exp[:], ACT.Copy, scale=-1.0).then_inc(a_ready, 1)
            ln_copies(1, 0)
            project_bc(0)
            project_rank(0)
            ln_copies(1, 1)
            for k in range(KC):
                project_abs(0, k)
                project_max(0, k)
            for k in range(KC):
                project_exp(0, k)
            ln_copies(1, 2)
            for k in range(KC):
                project_ln(0, k)
            ln_copies(1, 3)
            act.wait_ge(a_ready, 2)
            for b in range(BATCH):
                scan(b)
            ln_copies(2, BATCH - 1)
            route(1)
            shared(1)
            routed(1)

        @block.tensor
        def _(pe):
            def ln_transposes(c, b):
                for q in range(2 * b, 2 * b + 2):
                    pe.wait_ge(ln_xn, GT * c + 2 * q + 2)
                    if q >= 2:
                        pe.wait_ge(ln_xnT, (GT // 2) * c + q - 1)
                    if c == 2 and b + 2 < BATCH:
                        pe.wait_ge(pj_max, KC * (b + 3))
                    dst = (T, Y)[q % 2]
                    for i in range(2):
                        for k in range(KC):
                            last = nc.tensor.transpose(dst[:, (i * KC + k) * P:(i * KC + k + 1) * P],
                                                       xn[:, 2 * q + i, k * P:(k + 1) * P], ident[:])
                    last.then_inc(ln_tp, 1)

            def route(r, b):
                c = 2 * r
                if r == 1 and b == 0:
                    pe.wait_ge(sc_dbx, N * BATCH)
                    pe.wait_ge(sc_cc, N * BATCH)
                pe.wait_ge(ln_xnT, (GT // 2) * c + 2 * b + 2)
                for i in range(LT * b, LT * (b + 1)):
                    for k in range(KC):
                        last = nc.tensor.matmul(LG[:, i, :], xnT[:, k, i * P:(i + 1) * P], w_rt[:, k, :],
                                                start=(k == 0), stop=(k == KC - 1))
                last.then_inc(rt_logits, 1)

            def count(r):
                pe.wait_ge(rt_onehot, r + 1)
                flat = onehot[:].rearrange("p e i -> p (e i)")
                nc.tensor.matmul(YS[1][:, 0:E * GT], before[:], flat, start=True, stop=True)
                nc.tensor.matmul(YS[1][:, E * GT:2 * E * GT], ones[:], flat, start=True, stop=True).then_inc(rt_count, 1)

            def shared_down(r, b):
                pe.wait_ge(sh_hidden, 2 * (BATCH * r + b + 1))
                if b == 0:
                    pe.wait_ge(rt_read, r + 1)
                for q in range(LT * b, LT * (b + 1)):
                    if q >= 2:
                        pe.wait_ge(sh_x, GT * r + q - 1)
                    for k in range(KC):
                        last = nc.tensor.matmul(YS[q % 2][:, 0:D], sh_h[:, b % 2, k, (q % LT) * P:(q % LT + 1) * P],
                                                w_dn[:, k, SHARED, :], start=(k == 0), stop=(k == KC - 1))
                    last.then_inc(sh_y, 1)

            def shared(r):
                def gate_up(b, fo):
                    if b > 0:
                        pe.wait_ge(sh_hidden, 2 * (BATCH * r + b - 1) + fo + 1)
                    for w, dst in ((0, (H[0], T)[fo]), (F, (H[1], Y)[fo])):
                        for k in range(KC):
                            last = nc.tensor.matmul(dst[:, :], w_gu[:, k, SHARED, w + fo * P:w + (fo + 1) * P],
                                                    xnT[:, k, b * L:(b + 1) * L], start=(k == 0), stop=(k == KC - 1))
                    last.then_inc(sh_gu, 1)

                for b in range(BATCH):
                    gate_up(b, 0)
                    if b == 0:
                        count(r)
                    gate_up(b, 1)
                    if b > 0:
                        shared_down(r, b - 1)

            def routed(r):

                def gate_up(j0, i4=0):
                    e = pe.value_load(expert[0:1, bass.ds(j0 + i4, 1)], min_val=0, max_val=E - 1)
                    pe.wait_ge(ff_tpc, TS * r + j0 + 1 + i4)
                    if j0 >= 2:
                        pe.wait_ge(ff_hidden, NR * r + j0 - 1 + i4)
                    for k in range(KC):
                        last = nc.tensor.matmul(H[j0 % 2][:, :], tt[:, j0 % 2, 2 + k], w_gu[:, k, bass.ds(e, 1), :].squeeze(1),
                                                start=(k == 0), stop=(k == KC - 1))
                    last.then_inc(ff_gu, 1)

                def turn(j0, i4=0):
                    if j0 >= 0:
                        pe.wait_ge(ff_tpc, TS * r + j0 + 1 + i4)
                    if j0 >= 1:
                        pe.wait_ge(ff_hidden, NR * r + j0 + i4)
                        for k in range(KC):
                            last = nc.tensor.transpose(T[:, k * P:(k + 1) * P], h_sb[:, (j0 - 1) % 2, k * P:(k + 1) * P], ident[:])
                    if j0 + 1 < NR:
                        u = (j0 + 1) % 4
                        pe.wait_ge(ff_in[u], 16 * (uses(u) * r + (j0 + 1) // 4 + 1) + 4 * i4)
                        for k in range(KC):
                            last = nc.tensor.transpose(T[:, (2 + k) * P:(3 + k) * P], xg[:, u, k * P:(k + 1) * P], ident[:])
                    last.then_inc(ff_tp, 1)

                def down(j0, i4=0):
                    e = pe.value_load(expert[0:1, bass.ds(j0 + i4, 1)], min_val=0, max_val=E - 1)
                    pe.wait_ge(ff_tpc, TS * r + j0 + 3 + i4)
                    pe.wait_ge(ff_yc, 1 + NR * r + j0 + i4)
                    for k in range(KC):
                        last = nc.tensor.matmul(Y[:, 0:D], tt[:, j0 % 2, k], w_dn[:, k, bass.ds(e, 1), :].squeeze(1),
                                                start=(k == 0), stop=(k == KC - 1))
                    last.then_inc(ff_y, 1)

                pe.wait_ge(rt_expert, r + 1)
                if r == 0:
                    pe.wait_ge(experts_in, 16 * 3 * KC)
                pe.wait_ge(sh_hidden, 2 * BATCH * (r + 1))
                turn(-1)
                shared_down(r, BATCH - 1)
                gate_up(0)
                turn(0)
                gate_up(1)
                turn(1)
                with nc.Fori(0, NR - 6, 4, engines=[nc.tensor.engine]) as i4:
                    for j0 in range(2, 6):
                        gate_up(j0, i4)
                        turn(j0, i4)
                        down(j0 - 2, i4)
                gate_up(NR - 1)
                turn(NR - 1)
                down(NR - 3)
                turn(NR)
                down(NR - 2)
                down(NR - 1)

            def project_bc(b):
                lo = b * L
                pe.wait_ge(ln_xnT, GT // 2 + 2 * b + 2)
                if b == 1:
                    pe.wait_ge(ln_xnT, GT)
                if b > 1:
                    pe.wait_ge(ln_xnT, GT + 2 * (b - 2))
                    pe.wait_ge(pj_max, KC * b)
                for k in range(KC):
                    last = nc.tensor.matmul(pj_banks(b)[0][0:96, :], w_x[:, k, R:], xnT[:, k, lo:lo + L], start=(k == 0), stop=(k == KC - 1))
                last.then_inc(pj_bc, 1)

            def project_rank(b):
                lo = b * L
                for k in range(KC):
                    last = nc.tensor.matmul(pj_banks(b)[1][0:R, :], w_x[:, k, 0:R], xnT[:, k, lo:lo + L], start=(k == 0), stop=(k == KC - 1))
                last.then_inc(pj_rank, 1)

            def project_z(b):
                pe.wait_ge(pj_rankc, b + 1)
                pe.wait_ge(pj_split, b + 1)
                for k in range(KC):
                    nc.tensor.matmul(pj_banks(b)[k][:, :], w_dt[:, k * P:(k + 1) * P], rank_sb, start=True, stop=True).then_inc(pj_z, 1)

            def spread(b, n0, i2=0):
                s = N * b + n0 + i2
                u = n0 % 2
                if n0 + N * b == 0:
                    pe.wait_ge(pj_split, 1)
                if n0 == 0 and b > 0:
                    pe.wait_ge(pj_split, b + 1)
                for dst, m, used, signal in ((PB[u], 0, sc_dbx, sc_b), (PC[u], N, sc_cc, sc_c)):
                    if not (b == 0 and n0 < 2):
                        pe.wait_ge(used, s - 1)
                    nc.tensor.matmul(dst[:, :], pick[:, bass.ds(m + n0 + i2, 1)].to_broadcast([96, P]),
                                     bc_parts[:, b * L:(b + 1) * L], start=True, stop=True).then_inc(signal, 1)

            def scan(b):
                lo = b * L

                def add(n0, i2=0):
                    products = gs
                    if by_dve(b, n0):
                        products = dbx
                        pe.wait_ge(sc_last, n0 - (N - 3))
                    else:
                        pe.wait_ge(sc_g, N * b + n0 + 1 + i2)
                    for k in range(KC):
                        for i in range(LT):
                            last = nc.tensor.matmul(YA[k][:, i * P:(i + 1) * P], products[:, n0 % 2, k, i * P:(i + 1) * P], ident[:],
                                                    start=False, stop=(n0 == N - 1), is_transpose=True, skip_group_check=True)
                    last.then_inc(sc_tp, 1)

                def rounds(n0, count):
                    if count == 2:
                        for n in (n0, n0 + 1):
                            spread(b, n + 4)
                            add(n)
                        return
                    with nc.Fori(0, count - 1, 2, engines=[nc.tensor.engine]) as i2:
                        for u in range(2):
                            spread(b, n0 + u + 4, i2)
                            add(n0 + u, i2)

                if b > 0:
                    pe.wait_ge(sc_x, KC * b)
                pe.wait_ge(pj_xd, KC * (b + 1))
                for k in range(KC):
                    for i in range(LT):
                        nc.tensor.matmul(YA[k][:, i * P:(i + 1) * P], xnT[:, k, lo + i * P:lo + (i + 1) * P], ident[:],
                                         start=(i == 0), stop=False, is_transpose=True, skip_group_check=True)
                if b == 0:
                    spread(b, 3)
                rounds(0, 2)
                if b + 1 < BATCH:
                    project_bc(b + 1)
                    project_rank(b + 1)
                rounds(2, 2)
                spread(b, 8)
                add(4)
                if b + 1 < BATCH:
                    project_z(b + 1)
                rounds(5, 4)
                rounds(9, 2)
                spread(b, 15)
                add(11)
                if b > 0:
                    ln_transposes(2, b - 1)
                for u in range(4):
                    if b + 1 < BATCH:
                        spread(b + 1, u)
                    add(12 + u)

            pe.wait_ge(consts, 1)
            pe.wait_ge(router_in, 16)
            for b in range(BATCH):
                ln_transposes(0, b)
                if b > 0:
                    route(0, b - 1)
            route(0, BATCH - 1)
            pe.wait_ge(shared_in, 16 * 3)
            shared(0)
            routed(0)
            pe.wait_ge(ff_yc, 1 + NR)
            pe.wait_ge(small_in, 16 * 7)
            ln_transposes(1, 0)
            project_bc(0)
            project_rank(0)
            ln_transposes(1, 1)
            project_z(0)
            for b in range(2, BATCH):
                ln_transposes(1, b)
            pe.wait_ge(consts, 2)
            for n in range(3):
                spread(0, n)
            for b in range(BATCH):
                scan(b)
            for b in range(BATCH - 1):
                route(1, b)
            ln_transposes(2, BATCH - 1)
            route(1, BATCH - 1)
            shared(1)
            routed(1)

        @block.vector
        def _(dve):
            chain = [0]

            def link(ins):
                chain[0] += 1
                ins.then_inc(dve_chain, 1)
                dve.wait_ge(dve_chain, chain[0])

            def stats_of(c, b):
                for i in range(LT * b, LT * (b + 1)):
                    last = nc.vector.bn_stats(stats[:, i], x_sb[:, i, :])
                link(last)
                for i in range(LT * b, LT * (b + 1)):
                    last = nc.vector.bn_aggr(mv[:, i], stats[:, i])
                last.then_inc(ln_stats, 1)

            def normalise(c, b):
                dve.wait_ge(ln_stats, BATCH * c + b + 1)
                dve.wait_ge(ln_rstd, BATCH * c + b + 1)
                for i in range(LT * b, LT * (b + 1)):
                    nc.vector.tensor_scalar(xn[:, i], x_sb[:, i, :], mv[:, i, 0:1], rstd[:, i:i + 1],
                                            ALU.subtract, ALU.mult).then_inc(ln_xn, 1)

            def route(r):
                dve.wait_ge(rt_logits, BATCH * (r + 1))
                nc.vector.tensor_reduce(top[:], LG, AX.X, ALU.max).then_inc(rt_top, 1)
                dve.wait_ge(rt_top, r + 1)
                link(nc.vector.tensor_tensor(is_top[:], LG, top[:].unsqueeze(2).to_broadcast([P, GT, E]), ALU.is_equal))
                e_row = e_less[:].unsqueeze(1).to_broadcast([P, GT, E])
                link(nc.vector.tensor_tensor(cand[:], is_top[:], e_row, ALU.mult))
                link(nc.vector.tensor_reduce(first[:], cand[:], AX.X, ALU.min))
                nc.vector.tensor_tensor(onehot[:], e_less[:].unsqueeze(2).to_broadcast([P, E, GT]),
                                        first[:].unsqueeze(1).to_broadcast([P, E, GT]), ALU.is_equal).then_inc(rt_onehot, 1)
                dve.wait_ge(rt_count, r + 1)
                flat = "p e i -> p (e i)"
                link(nc.vector.tensor_tensor_scan(upto[:].rearrange(flat), keep[:].rearrange(flat),
                                                  COUNT.rearrange(flat), 0.0, ALU.mult, ALU.add))
                nc.vector.tensor_tensor(slot_m[:, 0], upto[:], COUNT, ALU.subtract)
                link(nc.vector.tensor_tensor(over[:], upto[:, :, GT - 1:GT].to_broadcast([P, E, GT]),
                                             tile_first[:].unsqueeze(1).to_broadcast([P, E, GT]), ALU.is_gt))
                nc.vector.tensor_tensor(slot_m[:, 1], slot_m[:, 0], RANK, ALU.add).then_inc(rt_read, 1)
                link(nc.vector.tensor_reduce(n_tiles[:], over[:], AX.X, ALU.add))
                link(nc.vector.tensor_tensor_scan(tiles_upto[:], ones_e[:], n_tiles[:], 0.0, ALU.mult, ALU.add))
                link(nc.vector.tensor_tensor(start_e[:, 0], tiles_upto[:], n_tiles[:], ALU.subtract))
                link(nc.vector.tensor_scalar(start_e[:, 1], start_e[:, 0], float(P), None, ALU.mult))
                link(nc.vector.tensor_tensor(slot_m[:, 2], slot_m[:, 1], start_e[:, 1].unsqueeze(2).to_broadcast([P, E, GT]), ALU.add))
                link(nc.vector.tensor_tensor(slot_m[:, 3], slot_m[:, 2], onehot[:], ALU.mult))
                link(nc.vector.tensor_reduce(slot_f[:], slot_m[:, 3].rearrange("p e i -> p i e"), AX.X, ALU.add))
                nc.vector.tensor_copy(slot[:], slot_f[:]).then_inc(rt_slot, 1)
                dve.wait_ge(rt_exp, r + 1)
                link(nc.vector.tensor_scalar(score[:, 1], score[:, 0], 1.0, None, ALU.add))
                link(nc.vector.reciprocal(score[:, 2], score[:, 1]))
                link(nc.vector.tensor_tensor(past, tiles_upto[:].unsqueeze(1).to_broadcast([P, NR, E]),
                                             tile_no[:].unsqueeze(2).to_broadcast([P, NR, E]), ALU.is_le))
                link(nc.vector.tensor_reduce(expert_f[:], past, AX.X, ALU.add))
                nc.vector.tensor_scalar(expert[:], expert_f[:], float(E - 1), None, ALU.min).then_inc(rt_expert, 1)

            def scale_rows(r, b):
                dve.wait_ge(ln_tp, (GT // 2) * 2 * r + 2 * b + 2)
                for i in range(LT * b, LT * (b + 1)):
                    last = nc.vector.tensor_scalar(xn[:, i], xn[:, i], score[:, 2, i:i + 1], None, ALU.mult)
                last.then_inc(rt_scaled, 1)

            def shared_result(r, b):
                for i in range(LT * b, LT * (b + 1)):
                    dve.wait_ge(sh_y, GT * r + i + 1)
                    nc.vector.scalar_tensor_tensor(out=x_sb[:, i], in0=YS[i % 2][:, 0:D], scalar=0.25, in1=x_sb[:, i],
                                                   op0=ALU.mult, op1=ALU.add).then_inc(sh_x, 1)

            def shared(r):
                for c2 in range(BATCH):
                    for fo in range(KC):
                        if c2 < 2:
                            scale_rows(r, KC * c2 + fo)
                        u = 2 * BATCH * r + 2 * c2 + fo
                        dve.wait_ge(sh_tanh, u + 1)
                        nc.vector.scalar_tensor_tensor(out=sh_q[:, fo], in0=sh_th[:, fo], scalar=1.0, in1=(H[0], T)[fo][:, :],
                                                       op0=ALU.add, op1=ALU.mult).then_inc(sh_mul, 1)
                        dve.wait_ge(sh_mul, u + 1)
                        nc.vector.tensor_tensor(sh_h[:, c2 % 2, fo], sh_q[:, fo], (H[1], Y)[fo][:, :], ALU.mult).then_inc(sh_hidden, 1)
                    if c2 > 0:
                        shared_result(r, c2 - 1)
                shared_result(r, BATCH - 1)

            def routed(r):
                def hidden(j0, i4=0):
                    u = j0 % 2
                    dve.wait_ge(ff_tanh, NR * r + j0 + 1 + i4)
                    nc.vector.scalar_tensor_tensor(out=q_sb[:, u], in0=th[:, u], scalar=1.0, in1=H[u][:, 0:F],
                                                   op0=ALU.add, op1=ALU.mult).then_inc(ff_mul, 1)
                    dve.wait_ge(ff_mul, NR * r + j0 + 1 + i4)
                    if j0 >= 2:
                        dve.wait_ge(ff_tp, TS * r + j0 + 1 + i4)
                    nc.vector.tensor_tensor(h_sb[:, u], q_sb[:, u], H[u][:, F:], ALU.mult).then_inc(ff_hidden, 1)

                def result(j0, i4=0):
                    u = j0 % 4
                    dve.wait_ge(ff_y, NR * r + j0 + 1 + i4)
                    if r > 0 or j0 >= 4:
                        dve.wait_ge(ff_out[u], 16 * (uses(u) * r + j0 // 4) + 4 * i4)
                    nc.vector.tensor_copy(y_sb[:, u], Y[:, 0:D]).then_inc(ff_yc, 1)

                for j in range(6):
                    hidden(j)
                    if j >= 2:
                        result(j - 2)
                with nc.Fori(0, NR - 10, 4, engines=[nc.vector.engine]) as i4:
                    for j0 in range(6, 10):
                        hidden(j0, i4)
                        result(j0 - 2, i4)
                hidden(NR - 1)
                result(NR - 3)
                result(NR - 2)
                result(NR - 1)

            def combine(r, b):
                if b == 0:
                    dve.wait_ge(sh_x, GT * (r + 1))
                dve.wait_ge(back_in[b], 16 * (r + 1))
                for i in range(LT * b, LT * (b + 1)):
                    nc.vector.scalar_tensor_tensor(out=x_sb[:, i], in0=xn[:, i], scalar=0.25, in1=x_sb[:, i],
                                                   op0=ALU.mult, op1=ALU.add).then_inc(back_x, 1)

            def project_split(b):
                ts = slice(b * L, (b + 1) * L)
                dve.wait_ge(pj_hi, b + 1)
                link(nc.vector.tensor_tensor(split_r[0:96], pj_banks(b)[0][0:96, :], bc_parts[:, ts], ALU.subtract))
                nc.vector.tensor_copy(bc_parts[32:64, ts], split_r[32:64])
                link(nc.vector.tensor_copy(mid_part[64:96], split_r[64:96]))
                nc.vector.tensor_tensor(bc_parts[64:96, ts], split_r[64:96], mid_part[64:96], ALU.subtract).then_inc(pj_split, 1)

            def project_w(b):
                dve.wait_ge(pj_exp, KC * (b + 1))
                nc.vector.tensor_scalar(sp_ln, sp_exp, 1.0, None, ALU.add).then_inc(pj_w, 1)

            def project_tmp(b):
                dve.wait_ge(pj_w, b + 1)
                nc.vector.scalar_tensor_tensor(out=sp_exp, in0=sp_ln, scalar=-1.0, in1=sp_exp, op0=ALU.add, op1=ALU.subtract).then_inc(pj_tmp, 1)
                dve.wait_ge(pj_max, KC * (b + 1))
                dve.wait_ge(pj_tmp, b + 1)
                link(nc.vector.tensor_tensor(dt_sb[:, :, seq(b)], dt_sb[:, :, seq(b)], sp_exp, ALU.subtract))

            def project_dt(b):
                dve.wait_ge(pj_ln, KC * (b + 1))
                if b > 0:
                    dve.wait_ge(pj_corr, 2 * b)
                nc.vector.tensor_tensor(dt_sb[:, :, seq(b)], dt_sb[:, :, seq(b)], sp_ln, ALU.add).then_inc(pj_dt, 1)
                dve.wait_ge(pj_dt, b + 1)
                nc.vector.tensor_tensor(dtx[:, :, seq(b)], dt_sb[:, :, seq(b)], xnT[:, :, b * L:(b + 1) * L], ALU.mult).then_inc(pj_dtx, 1)

            def product(b, n0, i2=0):
                s = N * b + n0 + i2
                if n0 == 0:
                    dve.wait_ge(pj_dtx, b + 1)
                dve.wait_ge(sc_b, s + 1)
                if not (b == 0 and n0 < 2):
                    dve.wait_ge(sc_h, KC * (s - 1))
                nc.vector.tensor_tensor(dbx[:, n0 % 2], dtx[:, :, seq(b)],
                                        PB[n0 % 2][:, :].unsqueeze(1).to_broadcast([P, KC, L]), ALU.mult).then_inc(sc_dbx, 1)

            def scan(b):
                def states(n0, i2=0):
                    s = N * b + n0 + i2
                    for k in range(KC):
                        dve.wait_ge(sc_dbx, s + 1)
                        if not (b == 0 and n0 < RING):
                            dve.wait_ge(sc_g, s - RING + 1)
                        dve.wait_ge(sc_da, KC * s + k + 1)
                        nc.vector.tensor_tensor_scan(ring(hs, n0, i2)[:, k], ring(da, n0, i2)[:, k], dbx[:, n0 % 2, k], 0.0, ALU.mult, ALU.add).then_inc(sc_h, 1)
                        if k == 0:
                            if n0 < N - 1:
                                product(b, n0 + 1, i2)
                            elif b + 1 < BATCH:
                                product(b + 1, 0)

                more = b + 1 < BATCH
                work = {1: b > 0, 4: more, 9: more, 11: b > 0, 13: more}
                for n0 in range(0, N, RING):
                    if 0 < n0 < N - RING and not any(work.get(n, False) for n in range(n0, n0 + RING)):
                        with nc.Fori(0, RING - 1, 2, engines=[nc.vector.engine]) as i2:
                            states(n0, i2)
                            states(n0 + 1, i2)
                        continue
                    for n in range(n0, n0 + RING):
                        states(n)
                        if b > 0 and n == 1:
                            add_y(b - 1)
                            dve.wait_ge(sc_x, KC * b)
                            stats_of(2, b - 1)
                        if more and n == 4:
                            project_split(b + 1)
                        if more and n == 9:
                            project_w(b + 1)
                        if b > 0 and n == 11:
                            normalise(2, b - 1)
                        if more and n == 13:
                            project_dt(b + 1)

            def last_products():
                b = BATCH - 1
                for n0 in range(N - 2, N):
                    dve.wait_ge(sc_h, KC * (N * b + n0 + 1))
                    dve.wait_ge(sc_cc, N * b + n0 + 1)
                    nc.vector.tensor_tensor(dbx[:, n0 % 2], hs[:, n0 % RING], c_sb[:, n0 % RING].unsqueeze(1).to_broadcast([P, KC, L]),
                                            ALU.mult).then_inc(sc_last, 1)

            def add_y(b):
                dve.wait_ge(sc_tp, N * (b + 1))
                for k in range(KC):
                    rows = x_sb[:, b * LT:(b + 1) * LT, k * P:(k + 1) * P]
                    nc.vector.tensor_tensor(rows, rows, YA[k][:, :].rearrange("p (i d) -> p i d", i=LT), ALU.add).then_inc(sc_x, 1)

            nc.vector.memset(first[:], 0.0).then_inc(ff_yc, 1)
            dve.wait_ge(consts, 1)
            for b in range(BATCH):
                dve.wait_ge(x_in[b], 16)
                stats_of(0, b)
                if b > 0:
                    normalise(0, b - 1)
            normalise(0, BATCH - 1)
            route(0)
            shared(0)
            routed(0)
            dve.wait_ge(small_in, 16 * 7)
            for b in range(BATCH):
                combine(0, b)
                dve.wait_ge(back_x, LT * (b + 1))
                stats_of(1, b)
                if b > 0:
                    normalise(1, b - 1)
                if b == 2:
                    project_split(0)
                if b == 3:
                    project_w(0)
                    project_tmp(0)
            normalise(1, BATCH - 1)
            project_dt(0)
            product(0, 0)
            for b in range(BATCH):
                scan(b)
            last_products()
            add_y(BATCH - 1)
            dve.wait_ge(sc_x, KC * BATCH)
            stats_of(2, BATCH - 1)
            normalise(2, BATCH - 1)
            route(1)
            shared(1)
            routed(1)
            for b in range(BATCH):
                combine(1, b)


_NAMES = ['x', 'W_x', 'W_dt', 'b_dt', 'A_log', 'D', 'router_w', 'gate_w', 'up_w', 'down_w',
          'shared_gate_w', 'shared_up_w', 'shared_down_w']


def kernel(**inputs):
    import numpy as np
    import concourse.bacc as bacc
    from concourse.bass_utils import run_bass_kernel_spmd

    nc = bacc.Bacc("TRN2", target_bir_lowering=False, num_devices=1)
    arrays, args = {}, []
    for name in _NAMES:
        full = next(k for k in inputs if k in ("L0_attn_" + name, "L0_ffn_" + name))
        a = np.asarray(inputs[full])
        if name in ("W_x", "W_dt"):
            a = a.T
        if name in ("b_dt", "D"):
            a = a.reshape(-1, P).T
        a = np.ascontiguousarray(a)
        arrays["in_" + name] = a
        args.append(nc.dram_tensor("in_" + name, a.shape, mybir.dt.from_np(a.dtype), kind="ExternalInput").ap())
    shape = np.asarray(inputs["L0_attn_x"]).shape
    out = nc.dram_tensor("out", shape, F32, kind="ExternalOutput").ap()
    macaron_kernel(nc, *args, out)
    r = run_bass_kernel_spmd(nc, [arrays], core_ids=[0])
    return r.results[0]["out"]
```
